# Optimizing a Trainium2 kernel written in Bass

```python
import numpy as np
import jax
import jax.numpy as jnp

def _softmax(x, axis=-1):
    return jax.nn.softmax(x, axis=axis)

def _gelu(x):
    return jax.nn.gelu(x, approximate=True)

def _silu(x):
    return jax.nn.silu(x)

def _sigmoid(x):
    return jax.nn.sigmoid(x)

def _layernorm(x, axis=-1, eps=1e-05):
    m = jnp.mean(x, axis=axis, keepdims=True)
    v = jnp.var(x, axis=axis, keepdims=True)
    return (x - m) / jnp.sqrt(v + eps)

def _scatter_add(tgt, idx, src, axis=0):
    return tgt.at[idx].add(src)

def _segment_sum(src, seg, n):
    return jax.ops.segment_sum(src, seg, n)
kernel_name = 'mk_prb_d2_jaxref_r4_139f95'

def setup_inputs(seed: int=0):
    np.random.seed(seed)
    _w = jnp.asarray

    def _L0_attn_setup():
        import jax, jax.numpy as jnp
        import numpy as np
        D_MODEL = 256
        NUM_HEADS = 16
        D_K = D_MODEL // NUM_HEADS
        key = jax.random.key(seed)
        k1, k2, k3, k4, k5 = jax.random.split(key, 5)
        scale = 1.0 / np.sqrt(D_MODEL)
        x = jax.random.normal(k1, (2, 2048, D_MODEL), dtype=jnp.float32)
        W_qkv = jax.random.normal(k2, (D_MODEL, 3 * D_MODEL), dtype=jnp.float32) * scale
        b_qkv = jax.random.normal(k3, (3 * D_MODEL,), dtype=jnp.float32) * 0.01
        W_out = jax.random.normal(k4, (D_MODEL, D_MODEL), dtype=jnp.float32) * scale
        b_out = jax.random.normal(k5, (D_MODEL,), dtype=jnp.float32) * 0.01
        return {'x': x, 'W_qkv': W_qkv, 'b_qkv': b_qkv, 'W_out': W_out, 'b_out': b_out}
    _L0_attn_in = _L0_attn_setup()

    def _L0_ffn_setup():
        import jax, jax.numpy as jnp
        import numpy as np
        D_MODEL = 256
        DEPTH = 8
        M = 2 ** DEPTH
        N_INTERNAL = M - 1
        B, T = (8, 1024)

        def _leaf_probs(gate):
            BT = gate.shape[0]
            lp = jnp.ones((BT, M), dtype=gate.dtype)
            for level in range(DEPTH):
                n = 2 ** level
                half = M // (2 * n)
                g = gate[:, n - 1:2 * n - 1]
                f = jnp.stack([1.0 - g, g], axis=-1)
                f = jnp.broadcast_to(f[..., None], (BT, n, 2, half))
                lp = lp * f.reshape(BT, M)
            return lp
        key = jax.random.key(seed)
        ks = jax.random.split(key, 7)
        x = jax.random.normal(ks[0], (B, T, D_MODEL), dtype=jnp.float32)
        Wq = jax.random.normal(ks[1], (D_MODEL, D_MODEL), dtype=jnp.float32) * 0.02
        routers = jax.random.normal(ks[2], (N_INTERNAL, D_MODEL), dtype=jnp.float32) * 0.02
        leaf_keys = jax.random.normal(ks[3], (M, D_MODEL), dtype=jnp.float32) * 0.02
        leaf_values = jax.random.normal(ks[4], (M, D_MODEL), dtype=jnp.float32) * 0.02
        Wout_w = jax.random.normal(ks[5], (D_MODEL, D_MODEL), dtype=jnp.float32) * 0.02
        Wout_b = jax.random.normal(ks[6], (D_MODEL,), dtype=jnp.float32) * 0.02
        return {'x': x, 'Wq': Wq, 'routers': routers, 'leaf_keys': leaf_keys, 'leaf_values': leaf_values, 'Wout_w': Wout_w, 'Wout_b': Wout_b}
    _L0_ffn_in = _L0_ffn_setup()

    def _L1_attn_setup():
        import jax, jax.numpy as jnp
        import numpy as np
        D_MODEL = 256
        NUM_HEADS = 16
        key = jax.random.key(seed)
        ks = jax.random.split(key, 5)
        B, T, d = (2, 512, D_MODEL)
        s = 1.0 / np.sqrt(d)
        return {'x': jax.random.normal(ks[0], (B, T, d), dtype=jnp.float32), 'W_kqv': jax.random.normal(ks[1], (d, 3 * d), dtype=jnp.float32) * s, 'b_kqv': jax.random.normal(ks[2], (3 * d,), dtype=jnp.float32) * 0.02, 'W_o': jax.random.normal(ks[3], (d, d), dtype=jnp.float32) * s, 'b_o': jax.random.normal(ks[4], (d,), dtype=jnp.float32) * 0.02}
    _L1_attn_in = _L1_attn_setup()

    def _L1_ffn_setup():
        import jax, jax.numpy as jnp
        import numpy as np
        TOP_K = 2
        key = jax.random.key(seed)
        ks = jax.random.split(key, 8)
        B, S, H, F, E = (1, 256, 256, 256, 8)
        Fs = 2 * F
        s = lambda k, shape, scale: jax.random.normal(k, shape, dtype=jnp.float32) * scale
        return {'x': s(ks[0], (B, S, H), 1.0), 'router_w': s(ks[1], (H, E), 0.02), 'gate_w': s(ks[2], (E, H, F), 0.02), 'up_w': s(ks[3], (E, H, F), 0.02), 'down_w': s(ks[4], (E, F, H), 0.02), 'shared_gate_w': s(ks[5], (H, Fs), 0.02), 'shared_up_w': s(ks[6], (H, Fs), 0.02), 'shared_down_w': s(ks[7], (Fs, H), 0.02)}
    _L1_ffn_in = _L1_ffn_setup()
    _d = {'L0_attn_x': _L0_attn_in['x'], 'L0_attn_W_qkv': _L0_attn_in['W_qkv'], 'L0_attn_b_qkv': _L0_attn_in['b_qkv'], 'L0_attn_W_out': _L0_attn_in['W_out'], 'L0_attn_b_out': _L0_attn_in['b_out'], 'L0_ffn_Wq': _L0_ffn_in['Wq'], 'L0_ffn_routers': _L0_ffn_in['routers'], 'L0_ffn_leaf_keys': _L0_ffn_in['leaf_keys'], 'L0_ffn_leaf_values': _L0_ffn_in['leaf_values'], 'L0_ffn_Wout_w': _L0_ffn_in['Wout_w'], 'L0_ffn_Wout_b': _L0_ffn_in['Wout_b'], 'L1_attn_W_kqv': _L1_attn_in['W_kqv'], 'L1_attn_b_kqv': _L1_attn_in['b_kqv'], 'L1_attn_W_o': _L1_attn_in['W_o'], 'L1_attn_b_o': _L1_attn_in['b_o'], 'L1_ffn_router_w': _L1_ffn_in['router_w'], 'L1_ffn_gate_w': _L1_ffn_in['gate_w'], 'L1_ffn_up_w': _L1_ffn_in['up_w'], 'L1_ffn_down_w': _L1_ffn_in['down_w'], 'L1_ffn_shared_gate_w': _L1_ffn_in['shared_gate_w'], 'L1_ffn_shared_up_w': _L1_ffn_in['shared_up_w'], 'L1_ffn_shared_down_w': _L1_ffn_in['shared_down_w']}
    _x0 = _d['L0_attn_x']
    _d['L0_attn_x'] = jax.random.normal(jax.random.fold_in(jax.random.key(seed), 1), (4, 1024, 256), dtype=_x0.dtype)
    del _x0
    return _d

def reference(L0_attn_x, L0_attn_W_qkv, L0_attn_b_qkv, L0_attn_W_out, L0_attn_b_out, L0_ffn_Wq, L0_ffn_routers, L0_ffn_leaf_keys, L0_ffn_leaf_values, L0_ffn_Wout_w, L0_ffn_Wout_b, L1_attn_W_kqv, L1_attn_b_kqv, L1_attn_W_o, L1_attn_b_o, L1_ffn_router_w, L1_ffn_gate_w, L1_ffn_up_w, L1_ffn_down_w, L1_ffn_shared_gate_w, L1_ffn_shared_up_w, L1_ffn_shared_down_w):

    def _L0_attn_ref(x, W_qkv, b_qkv, W_out, b_out):
        import jax, jax.numpy as jnp
        import numpy as np
        D_MODEL = 256
        NUM_HEADS = 16
        D_K = D_MODEL // NUM_HEADS
        B, S, _ = x.shape
        qkv = (jnp.einsum('bsd,de->bse', x, W_qkv) + b_qkv).reshape(B, S, NUM_HEADS, 3 * D_K)
        q, k, v = (qkv[..., :D_K], qkv[..., D_K:2 * D_K], qkv[..., 2 * D_K:])
        scores = jnp.einsum('bshd,bsgd->bshg', q, k) / np.sqrt(D_K)
        attn = jax.nn.softmax(scores, axis=-1)
        context = jnp.einsum('bshg,bsgd->bshd', attn, v).reshape(B, S, NUM_HEADS * D_K)
        return jnp.einsum('bsd,de->bse', context, W_out) + b_out

    def _L0_ffn_ref(x, Wq, routers, leaf_keys, leaf_values, Wout_w, Wout_b):
        import jax, jax.numpy as jnp
        import numpy as np
        D_MODEL = 256
        DEPTH = 8
        M = 2 ** DEPTH
        N_INTERNAL = M - 1
        B, T = (8, 1024)

        def _leaf_probs(gate):
            BT = gate.shape[0]
            lp = jnp.ones((BT, M), dtype=gate.dtype)
            for level in range(DEPTH):
                n = 2 ** level
                half = M // (2 * n)
                g = gate[:, n - 1:2 * n - 1]
                f = jnp.stack([1.0 - g, g], axis=-1)
                f = jnp.broadcast_to(f[..., None], (BT, n, 2, half))
                lp = lp * f.reshape(BT, M)
            return lp
        Bv, Tv, d = x.shape
        q = jnp.einsum('btd,ed->bte', x, Wq)
        q_flat = q.reshape(Bv * Tv, d)
        gate = jax.nn.sigmoid(q_flat @ routers.T)
        leaf_prob = _leaf_probs(gate)
        ret = (leaf_prob @ leaf_values).reshape(Bv, Tv, d)
        return jnp.einsum('btd,ed->bte', ret, Wout_w) + Wout_b

    def _L1_attn_ref(x, W_kqv, b_kqv, W_o, b_o):
        import jax, jax.numpy as jnp
        import numpy as np
        D_MODEL = 256
        NUM_HEADS = 16
        B, T, d = x.shape
        H = NUM_HEADS
        dk = d // H
        kqv = x @ W_kqv + b_kqv
        K, Q, V = jnp.split(kqv, 3, axis=-1)
        to_heads = lambda t: t.reshape(B, T, H, dk).transpose(0, 2, 1, 3)
        K, Q, V = (to_heads(K), to_heads(Q), to_heads(V))
        scores = jnp.einsum('bhtd,bhsd->bhts', Q, K)
        causal = jnp.triu(jnp.ones((T, T), dtype=bool), k=1)
        scores = jnp.where(causal, -jnp.inf, scores)
        attn = jax.nn.softmax(scores / jnp.sqrt(jnp.asarray(dk, x.dtype)), axis=-1)
        out = jnp.einsum('bhts,bhsd->bhtd', attn, V)
        out = out.transpose(0, 2, 1, 3).reshape(B, T, d)
        return out @ W_o + b_o

    def _L1_ffn_ref(x, router_w, gate_w, up_w, down_w, shared_gate_w, shared_up_w, shared_down_w):
        import jax, jax.numpy as jnp
        import numpy as np
        TOP_K = 2
        B, S, H = x.shape
        N = B * S
        xf = x.reshape(N, H)
        scores = jax.nn.softmax(xf @ router_w, axis=-1)
        topk_scores, topk_idx = jax.lax.top_k(scores, TOP_K)
        E = scores.shape[-1]
        combine = jnp.zeros((N, E), dtype=x.dtype).at[jnp.arange(N)[:, None], topk_idx].add(topk_scores)
        g = jnp.einsum('nh,ehf->enf', xf, gate_w)
        u = jnp.einsum('nh,ehf->enf', xf, up_w)
        y = jnp.einsum('enf,efh->enh', jax.nn.silu(g) * u, down_w)
        routed = jnp.einsum('enh,ne->nh', y, combine)
        shared = jax.nn.silu(xf @ shared_gate_w) * (xf @ shared_up_w) @ shared_down_w
        return (shared + routed).reshape(B, S, H)
    x = L0_attn_x
    xn = _layernorm(x, axis=-1)
    x = x + _L0_attn_ref(xn, L0_attn_W_qkv, L0_attn_b_qkv, L0_attn_W_out, L0_attn_b_out) + _L0_ffn_ref(xn, L0_ffn_Wq, L0_ffn_routers, L0_ffn_leaf_keys, L0_ffn_leaf_values, L0_ffn_Wout_w, L0_ffn_Wout_b)
    xn = _layernorm(x, axis=-1)
    x = x + _L1_attn_ref(xn, L1_attn_W_kqv, L1_attn_b_kqv, L1_attn_W_o, L1_attn_b_o) + _L1_ffn_ref(xn, L1_ffn_router_w, L1_ffn_gate_w, L1_ffn_up_w, L1_ffn_down_w, L1_ffn_shared_gate_w, L1_ffn_shared_up_w, L1_ffn_shared_down_w)
    return x

_drawn_inputs = setup_inputs


def setup_inputs(seed=0):
    import zlib

    import numpy as np

    out = dict(_drawn_inputs(seed))
    spreads = {}
    factors = {'L0_attn_b_qkv': 8.0,
     'L0_attn_b_out': 4.47,
     'L0_ffn_Wq': 8.0,
     'L0_ffn_routers': 8.0,
     'L0_ffn_leaf_values': 8.0,
     'L0_ffn_Wout_w': 8.0,
     'L1_attn_b_o': 24.042,
     'L1_ffn_router_w': 8.0,
     'L1_ffn_gate_w': 8.0,
     'L1_ffn_up_w': 8.0,
     'L1_ffn_down_w': 8.0,
     'L1_attn_W_kqv': 3.139,
     'L1_attn_b_kqv': 8.0,
     'L1_attn_W_o': 3.042,
     'L1_ffn_shared_gate_w': 8.0,
     'L1_ffn_shared_up_w': 8.0,
     'L1_ffn_shared_down_w': 8.0}
    for name, (base, spread) in spreads.items():
        noise = np.random.default_rng([zlib.crc32(name.encode()), seed]).standard_normal(out[name].shape)
        drawn = base * np.exp(spread * noise) if base else spread * noise
        out[name] = jnp.asarray(drawn.astype(out[name].dtype))
    for name, factor in factors.items():
        out[name] = (out[name] * factor).astype(out[name].dtype)
    return out
```

```python
from contextlib import ExitStack

import concourse.bass as bass
from concourse import mybir

F32 = mybir.dt.float32
BF16 = mybir.dt.bfloat16
ACT = mybir.ActivationFunctionType
ALU = mybir.AluOpType
AX = mybir.AxisListType

P = 128
B, T, D = 4, 1024, 256
N = B * T
NT = N // P
TB = T // P
KD = D // P
H, DK = 16, 16
NODE = 255
DEPTH = 8
E, ES = 8, 2
EA = E + ES
FF = 256
C = 512
NC_ = T // C
EPS = 1e-5
SCALE = 1.0 / DK ** 0.5
NEG = -1.0e30
LOWEST = -3.0e38
HP = 6
G4 = 4
NG = H // G4
PAIRS = [(0, 0), (0, 1), (1, 0), (1, 1), (0, 2), (2, 0)]
ROWS = len(PAIRS) * DK
ROWS_M = ROWS + 3


class Steps:

    def __init__(self, eng, sem):
        self.eng, self.sem, self.at, self.n, self.outer = eng, sem, 0, 0, []

    def did(self, instruction):
        instruction.then_inc(self.sem, 1)
        self.n += 1
        self.eng.wait_ge(self.sem, self.at + self.n)

    def enter(self, i, per):
        self.outer.append((self.at, self.n))
        self.at, self.n = self.at + self.n + i * per, 0

    def leave(self, count, per):
        assert self.n == per, (self.n, per)
        self.at, self.n = self.outer.pop()
        self.n += count * per


def wait(eng, sem, value):
    if isinstance(value, int) and value <= 0:
        return
    eng.wait_ge(sem, value)


def build(nc, x, w_qkv, b_qkv, w_out, b_out0, wq, routersT, leafT, woutT, wout_b, w_kqv, b_kqv, b_kq, w_o,
          b_o, router_w, w_gate, w_up, w_down, out):
    ctx = ExitStack()
    with ctx:
        def sb(name, shape, dt=F32):
            return ctx.enter_context(nc.sbuf_tensor(name, shape, dt))

        def sem(name):
            return ctx.enter_context(nc.semaphore(name))

        xs = sb("xs", [P, NT, D])
        wqkv_s = sb("wqkv_s", [P, KD, 3 * D])
        wout_s = sb("wout_s", [P, KD, D])
        rq_s = sb("rq_s", [P, KD, NODE + 1])
        lw_s = sb("lw_s", [P, KD, D])
        wkqv_s = sb("wkqv_s", [P, KD, 3 * D])
        wo_s = sb("wo_s", [P, KD, D])
        rw_s = sb("rw_s", [P, KD, E])
        brow = sb("brow", [1, 3 * D])
        brow_o = sb("brow_o", [1, 2, D])
        browv = sb("browv", [1, D])
        brow1 = sb("brow1", [1, D])
        bkq = sb("bkq", [P, 4])
        ones = sb("ones", [1, P])
        ident = sb("ident", [P, P])
        identb = sb("identb", [P, P], BF16)
        mask_n = sb("mask_n", [P, P], BF16)
        mask_t = sb("mask_t", [P, P], BF16)
        one = sb("one", [P, 1])
        pause = sb("pause", [P, 1])
        half = sb("half", [P, NT])
        st = sb("st", [P, NT, 6])
        mv = sb("mv", [P, NT, 2])
        rstd = sb("rstd", [P, NT])
        var = sb("var", [P, NT])
        arena = sb("arena", [P, 25600])
        free = [0]

        def take(words, shape, dt=F32):
            a = arena[:, free[0]:free[0] + words]
            free[0] += words
            if dt != F32:
                a = a.bitcast(dt)
            if len(shape) == 1:
                return a
            names = "abcd"[:len(shape)]
            return a.rearrange(f"p ({' '.join(names)}) -> p {' '.join(names)}",
                               **dict(zip(names[1:], shape[1:])))

        prod = take(H * H * DK, [H, H, DK])
        qkv = [take(3 * D, [H, 3, DK]) for _ in range(2)]
        gates = [take(NODE + 1, [NODE + 1]) for _ in range(2)]
        xn = [take(D, [D]) for _ in range(2)]
        xnT = [take(D, [KD, P]) for _ in range(2)]
        att = take(D, [H, H])
        prob = take(D, [H, H])
        mx = take(H, [H])
        sums = take(H, [H])
        ctx0 = [take(D, [H, DK]) for _ in range(2)]
        tree = [take(2 ** l, [2 ** l]) for l in range(1, DEPTH)]
        leaf = [take(D, [D // 2, 2]) for _ in range(2)]
        clT = [take(4 * P, [4, P]) for _ in range(2)]
        wq_s = take(KD * D, [KD, D])
        rT_s = take(KD * (NODE + 1), [KD, NODE + 1])
        lT_s = take(KD * D, [KD, D])
        wwT_s = take(KD * D, [KD, D])
        free[0] = 0
        QS = [take(G4 * T // 2, [G4, T], BF16) for _ in range(2)]
        KS = [take(G4 * T // 2, [G4, T], BF16) for _ in range(2)]
        PT = [take(G4 * C, [G4, C]) for _ in range(2)]
        vaug = take(TB * H * 32, [TB, H, 32])
        parts = [take(4 * T // 2, [4, T], BF16) for _ in range(3)]
        free[0] = 0
        w1 = [take(KD * 2 * FF, [KD, 2 * FF]) for _ in range(2)]
        w2 = [take(KD * D, [KD, D]) for _ in range(2)]
        cb = [take(T, [T]) for _ in range(2)]
        SG = [take(2 * C, [2, C]) for _ in range(2)]
        HM = take(2 * C, [2, C])
        HH = [take(2 * C, [2, C]) for _ in range(2)]
        YT = take(2 * T, [KD, NC_, C])

        xn2 = [sb(f"xn2_{i}", [P, D]) for i in range(2)]
        xbT = sb("xbT", [P, KD, T])
        XF = [sb(f"XF{i}", [P, C]) for i in range(2)]
        RR = sb("RR", [P, C])
        nmp = sb("nmp", [P, G4, TB, 2])
        nm = sb("nm", [P, TB, G4])
        nmr = sb("nmr", [P, TB, G4])
        nmb = sb("nmb", [P, TB, G4], BF16)
        ns = sb("ns", [P, TB, 3, G4])
        NR = sb("NR", [3 * G4, T], BF16)
        CA = sb("CA", [P, C])
        rc = sb("rc", [P, G4, G4])
        ctxN = sb("ctxN", [P, TB, D])
        cT = [sb(f"cT{i}", [P, KD, P]) for i in range(2)]
        LG = sb("LG", [P, TB, E])
        LP = sb("LP", [P, TB, E])
        CMB = sb("CMB", [P, TB, E])
        lmax = sb("lmax", [P, TB])
        lsum = sb("lsum", [P, TB])
        top8 = sb("top8", [P, TB, 8])
        rep8 = sb("rep8", [P, TB, 8])
        cT8 = sb("cT8", [EA, T])

        PS = ctx.enter_context(nc.psum_tensor("PS", [P, 8, C], F32))

        scr_parts = nc.dram_tensor("scr_parts", (3, 4, P, T), BF16).ap()
        scr_neg = nc.dram_tensor("scr_neg", (3, G4, T), BF16).ap()
        scr_cmb = nc.dram_tensor("scr_cmb", (EA, T), F32).ap()

        s = {name: sem(name) for name in (
            "tanh_done w_first x_loaded w_loaded const_done rows_ready var_ready rstd_ready d_step p_step "
            "fold_done fold_ready xn_ready xT_done xT_ready proj_done qkv_ready gate_ready "
            "mulp_done part_reduced shifted probs_ready leaf_ready ctx_ready backT_done back_ready "
            "out_done x2_done "
            "ln_ready lnT_done xbT_ready kq_done kq_evac parts_ready parts_stored v_done v_evac "
            "cmb_ready cmbT_done cmbT_ready cmb_stored stack0 stack1 neg0 neg1 a_scored a_maxed "
            "ns_ready nsT_done nr_ready n_stored s_scored p_ready pv_done c_evac ctxT_done cn_done "
            "woT_done wo_ready wo_done wo_added "
            "ew0 ew1 g_done u_done silu_done h_ready y_done y_evac yT_done y_added stored").split()}
        stack, neg, ew = [s["stack0"], s["stack1"]], [s["neg0"], s["neg1"]], [s["ew0"], s["ew1"]]

        steps = [(qc, kt) for qc in range(NC_) for kt in range(4 * (qc + 1))]
        units = [(hh, i, part) for hh in range(G4) for i in range(TB) for part in range(1 + (i >= 4))]
        NS_, NU = len(steps), len(units)

        def schedule():
            order = [("A", 0, u) for u in range(NU)] + [("N", 0, 0)]
            pending = None
            for g in range(NG):
                order.append(("S", g, 0))
                for t in range(NS_):
                    if g + 1 < NG:
                        per = NU // 8
                        order += [("A", g + 1, u) for u in range(per * t, min(NU, per * t + per))]
                        if t == 8:
                            order.append(("N", g + 1, 0))
                    if t + 1 < NS_:
                        order.append(("S", g, t + 1))
                    order.append(("PV", g, t))
                    if pending:
                        order.append(pending)
                        pending = None
                    if t + 1 == NS_ or steps[t + 1][0] != steps[t][0]:
                        order.append(("CE", g, steps[t][0]))
                        pending = ("CT", g, steps[t][0])
            return order + [pending]

        ORDER = schedule()

        def q_span(qc, kt):
            first = max(qc * C, kt * P)
            return first, (qc + 1) * C - first

        block = ctx.enter_context(nc.Block())

        @block.sync
        def _(sp):
            for dst, src in ((wq_s, wq), (rT_s[:, :, 0:NODE], routersT), (lT_s, leafT), (wwT_s, woutT)):
                sp.dma_start(dst, src.rearrange("(k p) n -> p k n", p=P)).then_inc(s["w_first"], 16)
            xv = x.rearrange("(n p) d -> p n d", p=P)
            for b in range(B):
                sp.dma_start(xs[:, b * TB:(b + 1) * TB, :], xv[:, b * TB:(b + 1) * TB, :]).then_inc(s["x_loaded"], 16)
            for dst, src in ((wqkv_s, w_qkv), (wout_s, w_out), (wkqv_s, w_kqv), (wo_s, w_o), (rw_s, router_w)):
                sp.dma_start(dst[:, :, :], src.rearrange("(k p) n -> p k n", p=P)).then_inc(s["w_loaded"], 16)
            row = lambda a: a.rearrange("(o n) -> o n", o=1)
            sp.dma_start(brow[:, :], row(b_qkv)).then_inc(s["w_loaded"], 16)
            sp.dma_start(brow_o[:, 0, :], row(b_out0)).then_inc(s["w_loaded"], 16)
            sp.dma_start(brow_o[:, 1, :], row(wout_b)).then_inc(s["w_loaded"], 16)
            sp.dma_start(browv[:, :], row(b_kqv)[:, 2 * D:3 * D]).then_inc(s["w_loaded"], 16)
            sp.dma_start(brow1[:, :], row(b_o)).then_inc(s["w_loaded"], 16)
            sp.dma_start(bkq[:, :], b_kq).then_inc(s["w_loaded"], 16)

            with sp.Fori(0, B) as b:
                sp.wait_ge(s["parts_ready"], b * 8 + 8)
                for p in range(3):
                    sp.dma_start(scr_parts[p].rearrange("m p t -> p m t"), parts[p]).then_inc(s["parts_stored"], 16)
                sp.wait_ge(s["cmbT_ready"], b * 2 + 2)
                sp.dma_start(scr_cmb, cT8[:, :]).then_inc(s["cmb_stored"], 16)
                sp.wait_ge(s["parts_stored"], b * 48 + 48)

                def load_stack(g):
                    sp.wait_ge(s["pv_done"], b * (NG * NS_) + NS_ * max(0, g - 1))
                    for stackd, base, side in ((KS, 0, 1), (QS, 2, 0)):
                        for r, pair in enumerate(PAIRS):
                            p0 = (g % 2) * G4 * DK
                            src = scr_parts[pair[side], base + g // 2, p0:p0 + G4 * DK, :]
                            sp.dma_start(stackd[g % 2][r * DK:(r + 1) * DK, :, :],
                                         src.rearrange("(h d) t -> d h t", d=DK)).then_inc(stack[g % 2], 16)

                def load_neg(g):
                    sp.wait_ge(s["nr_ready"], b * 2 * NG + 2 * g + 2)
                    sp.dma_start(scr_neg.rearrange("p h t -> (p h) t"), NR[:, :]).then_inc(s["n_stored"], 16)
                    sp.wait_ge(s["n_stored"], (b * NG + g + 1) * 16)
                    sp.dma_start(QS[g % 2][ROWS:ROWS_M, :, :], scr_neg).then_inc(neg[g % 2], 16)

                load_stack(0)
                load_stack(1)
                load_neg(0)
                load_neg(1)
                load_stack(2)
                load_neg(2)
                load_stack(3)
                load_neg(3)

                sp.wait_ge(s["pv_done"], (b + 1) * (NG * NS_))
                sp.wait_ge(s["cmb_stored"], b * 16 + 16)

                def load_expert(e, slot):
                    sp.dma_start(w1[slot][:, :, 0:FF], w_gate[bass.ds(e, 1), :, :].rearrange("o (k p) n -> p (o k) n", p=P)).then_inc(ew[slot], 16)
                    sp.dma_start(w1[slot][:, :, FF:2 * FF], w_up[bass.ds(e, 1), :, :].rearrange("o (k p) n -> p (o k) n", p=P)).then_inc(ew[slot], 16)
                    sp.dma_start(w2[slot], w_down[bass.ds(e, 1), :, :].rearrange("o (k p) n -> p (o k) n", p=P)).then_inc(ew[slot], 16)
                    sp.dma_start(cb[slot], scr_cmb[bass.ds(e, 1), :].partition_broadcast(P).rearrange("p o t -> p (o t)")).then_inc(ew[slot], 16)

                load_expert(0, 0)
                load_expert(1, 1)
                with sp.Fori(1, EA // 2) as k:
                    for slot in range(2):
                        sp.wait_ge(s["y_done"], b * (2 * EA) + k * 4 + (2 * slot - 2))
                        load_expert(k * 2 + slot, slot)

                sp.wait_ge(s["y_added"], b * TB + TB)
                ov = out.rearrange("(b n p) d -> b p n d", p=P, b=B)
                sp.dma_start(ov[bass.ds(b, 1), :, :, :].rearrange("o p n d -> p (o n) d"),
                             xs[:, bass.ds(b * TB, TB), :]).then_inc(s["stored"], 16)
            sp.wait_ge(s["stored"], B * 16)

        @block.gpsimd
        def _(pool):
            step = Steps(pool, s["p_step"])
            step.did(nc.gpsimd.memset(ident[:, :], 0.0))
            step.did(nc.gpsimd.affine_select(out=ident[:, :], in_=ident[:, :], compare_op=ALU.not_equal, fill=1.0,
                                             base=0, pattern=[[-1, P]], channel_multiplier=1))
            nc.gpsimd.memset(ones[:, :], 1.0)
            nc.gpsimd.memset(one[:, :], 1.0)
            step.did(nc.gpsimd.memset(half[:, :], -0.5))
            step.did(nc.gpsimd.memset(mask_n[:, :], 0.0))
            step.did(nc.gpsimd.memset(mask_t[:, :], 0.0))
            step.did(nc.gpsimd.affine_select(out=mask_n[:, :], in_=mask_n[:, :], compare_op=ALU.is_ge, fill=NEG,
                                             base=0, pattern=[[-1, P]], channel_multiplier=1))
            step.did(nc.gpsimd.affine_select(out=mask_t[:, :], in_=mask_t[:, :], compare_op=ALU.is_ge, fill=NEG,
                                             base=0, pattern=[[1, P]], channel_multiplier=-1))
            nc.gpsimd.tensor_scalar(identb[:, :], ident[:, :], 1.0, None, ALU.mult).then_inc(s["const_done"], 1)
            pool.wait_ge(s["var_ready"], 1)
            nc.gpsimd.tensor_tensor(rstd[:, :], var[:, :], half[:, :], ALU.pow).then_inc(s["rstd_ready"], 1)

            def first(n, sl):
                t = qkv[sl]
                q, k, v = t[:, :, 0, :], t[:, :, 1, :], t[:, :, 2, :]
                pool.wait_ge(s["qkv_ready"], n + 1)
                wait(pool, s["part_reduced"], n * 2)
                nc.gpsimd.tensor_tensor(prod[:, 0:HP, :, :], q[:, 0:HP, :].unsqueeze(2).to_broadcast([P, HP, H, DK]),
                                        k.unsqueeze(1).to_broadcast([P, HP, H, DK]), ALU.mult).then_inc(s["mulp_done"], 1)
                pool.wait_ge(s["gate_ready"], n + 1)
                if not (isinstance(n, int) and n < 2):
                    pool.wait_ge(s["backT_done"], n - 1)
                g = gates[sl]
                nc.gpsimd.tensor_tensor(tree[0][:, 0:1], one[:, :], g[:, 0:1], ALU.subtract)
                step.did(nc.gpsimd.tensor_tensor(tree[0][:, 1:2], one[:, :], g[:, 0:1], ALU.mult))
                for l in range(1, DEPTH):
                    m = 2 ** l
                    to = leaf[sl] if l == DEPTH - 1 else tree[l].rearrange("p (n c) -> p n c", c=2)
                    step.did(nc.gpsimd.tensor_tensor(to[:, :, 1], tree[l - 1], g[:, m - 1:2 * m - 1], ALU.mult))
                    i = nc.gpsimd.tensor_tensor(to[:, :, 0], tree[l - 1], to[:, :, 1], ALU.subtract)
                    if l < DEPTH - 1:
                        step.did(i)
                    else:
                        i.then_inc(s["leaf_ready"], 1)
                pool.wait_ge(s["probs_ready"], n + 1)
                pool.wait_ge(s["part_reduced"], n * 2 + 1)
                nc.gpsimd.tensor_tensor(prod[:, 0:HP, :, :], prob[:, 0:HP, :].unsqueeze(2).to_broadcast([P, HP, DK, H]),
                                        v.rearrange("p g d -> p d g").unsqueeze(1).to_broadcast([P, HP, DK, H]),
                                        ALU.mult).then_inc(s["mulp_done"], 1)

            per = 1 + 2 * (DEPTH - 2) + 1
            first(0, 0)
            first(1, 1)
            with pool.Fori(1, NT // 2) as k:
                step.enter(k - 1, 2 * per)
                first(k * 2, 0)
                first(k * 2 + 1, 1)
                step.leave(NT // 2 - 1, 2 * per)
            with pool.Fori(0, B) as b:
                pool.wait_ge(s["var_ready"], b + 2)
                nc.gpsimd.tensor_tensor(rstd[:, 0:TB], var[:, 0:TB], half[:, 0:TB], ALU.pow).then_inc(s["rstd_ready"], 1)

        @block.vector
        def _(dve):
            V = nc.vector
            step = Steps(dve, s["d_step"])
            V.memset(nmp[:, :, :, :], LOWEST)
            V.memset(rep8[:, :, :], -1.0)
            V.memset(cT8[:, :], 1.0).then_inc(s["rows_ready"], 1)
            dve.wait_ge(s["x_loaded"], B * 16)

            def norm_stats(tiles, at):
                for j in range(tiles):
                    ins = V.bn_stats(st[:, j, :], xs[:, at(j), :])
                step.did(ins)
                V.memset(pause[:, :], 0.0)
                for j in range(tiles):
                    ins = V.bn_aggr(mv[:, j, :], st[:, j, :])
                step.did(ins)
                V.tensor_scalar(var[:, 0:tiles], mv[:, 0:tiles, 1], EPS, None, ALU.add).then_inc(s["var_ready"], 1)

            norm_stats(NT, lambda j: j)
            dve.wait_ge(s["rstd_ready"], 1)

            dve.wait_ge(s["fold_done"], 1)
            V.tensor_copy(rq_s[:, :, 0:NODE], PS[:, 0:2, 0:NODE])
            V.tensor_copy(lw_s[:, :, :], PS[:, 2:4, 0:D]).then_inc(s["fold_ready"], 1)

            def normed(n, sl):
                if not (isinstance(n, int) and n < 2):
                    dve.wait_ge(s["xT_done"], n - 1)
                V.tensor_scalar(xn[sl], xs[:, n, :], mv[:, n, 0:1], rstd[:, bass.ds(n, 1)] if not isinstance(n, int) else rstd[:, n:n + 1],
                                ALU.subtract, ALU.mult).then_inc(s["xn_ready"], 1)

            def attend(n, sl):
                t = qkv[sl]
                q, k, v = t[:, :, 0, :], t[:, :, 1, :], t[:, :, 2, :]
                own = H - HP
                dve.wait_ge(s["qkv_ready"], n + 1)
                step.did(V.tensor_tensor(prod[:, HP:H, :, :], q[:, HP:H, :].unsqueeze(2).to_broadcast([P, own, H, DK]),
                                         k.unsqueeze(1).to_broadcast([P, own, H, DK]), ALU.mult))
                V.tensor_reduce(att[:, HP:H, :], prod[:, HP:H, :, :], AX.X, ALU.add)
                dve.wait_ge(s["mulp_done"], n * 2 + 1)
                i = V.tensor_reduce(att[:, 0:HP, :], prod[:, 0:HP, :, :], AX.X, ALU.add)
                i.then_inc(s["part_reduced"], 1)
                dve.wait_ge(s["part_reduced"], n * 2 + 1)
                step.did(V.tensor_reduce(mx, att, AX.X, ALU.max))
                V.tensor_tensor(att, att, mx.unsqueeze(2).to_broadcast([P, H, H]), ALU.subtract).then_inc(s["shifted"], 1)
                dve.wait_ge(s["probs_ready"], n + 1)
                step.did(V.tensor_reduce(sums, prob, AX.X, ALU.add))
                V.reciprocal(mx, sums)
                step.did(V.tensor_tensor(prod[:, HP:H, :, :], prob[:, HP:H, :].unsqueeze(2).to_broadcast([P, own, DK, H]),
                                         v.rearrange("p g d -> p d g").unsqueeze(1).to_broadcast([P, own, DK, H]), ALU.mult))
                V.tensor_reduce(att[:, HP:H, :], prod[:, HP:H, :, :], AX.X, ALU.add)
                dve.wait_ge(s["mulp_done"], n * 2 + 2)
                V.tensor_reduce(att[:, 0:HP, :], prod[:, 0:HP, :, :], AX.X, ALU.add).then_inc(s["part_reduced"], 1)
                dve.wait_ge(s["part_reduced"], n * 2 + 2)
                if not (isinstance(n, int) and n < 2):
                    dve.wait_ge(s["backT_done"], n - 1)
                V.tensor_tensor(ctx0[sl], att, mx.unsqueeze(2).to_broadcast([P, H, DK]), ALU.mult).then_inc(s["ctx_ready"], 1)

            def update(n, sl):
                dve.wait_ge(s["out_done"], n + 1)
                V.tensor_tensor(xs[:, n, :], PS[:, 6 + sl, 0:D], xs[:, n, :], ALU.add).then_inc(s["x2_done"], 1)

            per = 4
            normed(0, 0)
            normed(1, 1)
            attend(0, 0)
            with dve.Fori(0, NT // 2 - 1) as k:
                step.enter(k, 2 * per)
                normed(k * 2 + 2, 0)
                attend(k * 2 + 1, 1)
                update(k * 2, 0)
                normed(k * 2 + 3, 1)
                attend(k * 2 + 2, 0)
                update(k * 2 + 1, 1)
                step.leave(NT // 2 - 1, 2 * per)
            attend(NT - 1, 1)
            update(NT - 2, 0)
            update(NT - 1, 1)
            dve.wait_ge(s["x2_done"], NT)

            def batch(b):
                dve.wait_ge(s["y_added"], b * TB)
                V.memset(vaug[:, :, :, DK:32], 1.0)
                for sl in range(2):
                    V.memset(KS[sl][ROWS:ROWS_M, :, :], 1.0)
                norm_stats(TB, lambda j: b * TB + j)
                dve.wait_ge(s["rstd_ready"], b + 2)
                for j in range(TB):
                    if j >= 2:
                        dve.wait_ge(s["lnT_done"], b * TB + (j - 1))
                    V.tensor_scalar(xn2[j % 2][:, :], xs[:, b * TB + j, :], mv[:, j, 0:1], rstd[:, j:j + 1],
                                    ALU.subtract, ALU.mult).then_inc(s["ln_ready"], 1)
                for u in range(8):
                    blk, c = divmod(u, 2)
                    to = [a[:, blk, c * C:(c + 1) * C] for a in parts]
                    dve.wait_ge(s["kq_evac"], b * 8 + u + 1)
                    if u == 0:
                        wait(dve, s["parts_stored"], b * 48)
                    step.did(V.tensor_copy(to[0], XF[u % 2][:, :]))
                    step.did(V.tensor_tensor(RR[:, :], XF[u % 2][:, :], to[0], ALU.subtract))
                    step.did(V.tensor_copy(to[1], RR[:, :]))
                    V.tensor_tensor(to[2], RR[:, :], to[1], ALU.subtract).then_inc(s["parts_ready"], 1)
                dve.wait_ge(s["v_evac"], b * TB + TB)
                step.did(V.tensor_reduce(lmax[:, :], LG[:, :, :], AX.X, ALU.max))
                V.tensor_tensor(LP[:, :, :], LG[:, :, :], lmax[:, :].unsqueeze(2).to_broadcast([P, TB, E]),
                                ALU.subtract).then_inc(s["shifted"], 1)
                dve.wait_ge(s["probs_ready"], b + NT + 1)
                step.did(V.tensor_reduce(lsum[:, :], LP[:, :, :], AX.X, ALU.add))
                step.did(V.reciprocal(lmax[:, :], lsum[:, :]))
                step.did(V.tensor_tensor(LP[:, :, :], LP[:, :, :], lmax[:, :].unsqueeze(2).to_broadcast([P, TB, E]), ALU.mult))
                V.memset(pause[:, :], 0.0)
                for j in range(TB):
                    ins = V.max(top8[:, j, :], LP[:, j, :])
                step.did(ins)
                step.did(V.tensor_copy(rep8[:, :, 0:2], top8[:, :, 0:2]))
                V.memset(pause[:, :], 0.0)
                for j in range(TB):
                    ins = V.match_replace(out=CMB[:, j, :], in_to_replace=rep8[:, j, :], in_values=LP[:, j, :], imm_value=0.0)
                step.did(ins)
                V.tensor_tensor(CMB[:, :, :], LP[:, :, :], CMB[:, :, :], ALU.subtract).then_inc(s["cmb_ready"], 1)

                for kind, g, u in ORDER:
                    if kind == "A":
                        hh, i, part = units[u]
                        w = min(C, (i + 1) * P - part * C)
                        dve.wait_ge(s["a_scored"], b * (NG * NU) + g * NU + u + 1)
                        V.tensor_reduce(nmp[:, hh, i, part:part + 1], PS[:, u % 2, 0:w], AX.X, ALU.max).then_inc(s["a_maxed"], 1)
                    elif kind == "N":
                        dve.wait_ge(s["a_maxed"], b * (NG * NU) + (g + 1) * NU)
                        wait(dve, s["nsT_done"], b * (2 * NG) + 2 * g)
                        step.did(V.tensor_reduce(nm[:, :, :].rearrange("p i h -> p h i"), nmp[:, :, :, :], AX.X, ALU.max))
                        step.did(V.tensor_scalar(nm[:, :, :], nm[:, :, :], -1.0, None, ALU.mult))
                        step.did(V.tensor_copy(nmb[:, :, :], nm[:, :, :]))
                        V.tensor_copy(ns[:, :, 0, :], nmb[:, :, :])
                        step.did(V.tensor_tensor(nmr[:, :, :], nm[:, :, :], nmb[:, :, :], ALU.subtract))
                        step.did(V.tensor_copy(nmb[:, :, :], nmr[:, :, :]))
                        V.tensor_copy(ns[:, :, 1, :], nmb[:, :, :])
                        V.tensor_tensor(ns[:, :, 2, :], nmr[:, :, :], nmb[:, :, :], ALU.subtract).then_inc(s["ns_ready"], 1)
                    elif kind == "CT":
                        k = 2 * g + u
                        dve.wait_ge(s["ctxT_done"], b * (2 * NG) + k + 1)
                        got = PS[:, 2, :].rearrange("p (q h e) -> p q h e", q=4, h=G4)
                        step.did(V.reciprocal(rc[:, :, :], got[:, :, :, DK]))
                        V.tensor_tensor(ctxN[:, 4 * u:4 * u + 4, g * G4 * DK:(g + 1) * G4 * DK].rearrange("p q (h d) -> p q h d", d=DK),
                                        got[:, :, :, 0:DK], rc[:, :, :].unsqueeze(3).to_broadcast([P, 4, G4, DK]),
                                        ALU.mult).then_inc(s["cn_done"], 1)
                for j in range(TB):
                    dve.wait_ge(s["wo_done"], b * TB + j + 1)
                    V.tensor_tensor(xs[:, b * TB + j, :], PS[:, 4 + j % 2, 0:D], xs[:, b * TB + j, :], ALU.add).then_inc(s["wo_added"], 1)

                def hidden(v, par, e_slot, k, c):
                    dve.wait_ge(ew[e_slot], (b * 5 + k + 1) * 64)
                    dve.wait_ge(s["silu_done"], b * 20 + v + 1)
                    dve.wait_ge(s["h_ready"], b * 20 + v)
                    step.did(V.tensor_tensor(HM, SG[par], cb[e_slot][:, c * C:(c + 1) * C].unsqueeze(1).to_broadcast([P, 2, C]), ALU.mult))
                    dve.wait_ge(s["u_done"], b * 20 + v + 1)
                    wait(dve, s["y_done"], b * 20 + v - 1 if not isinstance(v, int) or v >= 2 else b * 20)
                    V.tensor_tensor(HH[par], HM, PS[:, 2:4, :], ALU.mult).then_inc(s["h_ready"], 1)

                for v in range(4):
                    hidden(v, v % 2, v // 2, 0, v % 2)
                with dve.Fori(1, EA // 2) as k:
                    step.enter(k - 1, 4)
                    for v in range(4):
                        hidden(k * 4 + v, v % 2, v // 2, k, v % 2)
                    step.leave(EA // 2 - 1, 4)
                for j in range(TB):
                    dve.wait_ge(s["yT_done"], b * TB + j + 1)
                    V.tensor_tensor(xs[:, b * TB + j, :], PS[:, j % 2, 0:D], xs[:, b * TB + j, :], ALU.add).then_inc(s["y_added"], 1)

            PER_B = 2 + 24 + 4 + 3 + NG * 5 + 2 * NG + 2 * EA
            with dve.Fori(0, B) as b:
                step.enter(b, PER_B)
                batch(b)
                step.leave(B, PER_B)

        @block.scalar
        def _(act):
            A = nc.scalar

            def front(n, sl):
                act.wait_ge(s["xT_done"], n + 1)
                A.copy(xnT[sl], PS[:, 4, 0:D].rearrange("p (k t) -> p k t", k=KD)).then_inc(s["xT_ready"], 1)
                act.wait_ge(s["proj_done"], n + 1)
                if not (isinstance(n, int) and n < 2):
                    act.wait_ge(s["ctx_ready"], n - 1)
                    act.wait_ge(s["mulp_done"], n * 2 - 2)
                    act.wait_ge(s["leaf_ready"], n - 1)
                t = qkv[sl].rearrange("p h c d -> p (h c d)")
                A.copy(t[:, 0:C], PS[:, sl, :])
                A.copy(t[:, C:3 * D], PS[:, 2 + sl, 0:3 * D - C]).then_inc(s["qkv_ready"], 1)
                A.activation(gates[sl][:, 0:NODE], PS[:, 2 + sl, D:D + NODE], ACT.Tanh, scale=0.5).then_inc(s["tanh_done"], 1)
                act.wait_ge(s["tanh_done"], n + 1)
                A.activation(gates[sl][:, 0:NODE], gates[sl][:, 0:NODE], ACT.Copy, scale=0.5, bias=0.5).then_inc(s["gate_ready"], 1)

            def exps(n):
                act.wait_ge(s["shifted"], n + 1)
                wait(act, s["ctx_ready"], n)
                A.activation(prob, att, ACT.Exp, scale=SCALE).then_inc(s["probs_ready"], 1)

            def back(n, sl):
                act.wait_ge(s["backT_done"], n + 1)
                A.copy(clT[sl], PS[:, 5, :].rearrange("p (k t) -> p k t", k=4)).then_inc(s["back_ready"], 1)

            front(0, 0)
            with act.Fori(0, NT // 2 - 1) as k:
                front(k * 2 + 1, 1)
                exps(k * 2)
                back(k * 2, 0)
                front(k * 2 + 2, 0)
                exps(k * 2 + 1)
                back(k * 2 + 1, 1)
            front(NT - 1, 1)
            exps(NT - 2)
            back(NT - 2, 0)
            exps(NT - 1)
            back(NT - 1, 1)

            with act.Fori(0, B) as b:
                for j in range(TB):
                    act.wait_ge(s["lnT_done"], b * TB + j + 1)
                    A.copy(xbT[:, :, j * P:(j + 1) * P], PS[:, 4 + j % 2, 0:D].rearrange("p (k t) -> p k t", k=KD)).then_inc(s["xbT_ready"], 1)
                for u in range(8):
                    act.wait_ge(s["kq_done"], b * 8 + u + 1)
                    wait(act, s["parts_ready"], b * 8 + max(0, u - 1))
                    A.activation(XF[u % 2][:, :], PS[:, u % 4, :], ACT.Identity, bias=bkq[:, u // 2:u // 2 + 1]).then_inc(s["kq_evac"], 1)
                for j in range(TB):
                    act.wait_ge(s["v_done"], b * TB + j + 1)
                    A.copy(vaug[:, j, :, 0:DK], PS[:, 4 + j % 2, 0:D].rearrange("p (h d) -> p h d", d=DK))
                    A.copy(LG[:, j, :], PS[:, 4 + j % 2, D:D + E]).then_inc(s["v_evac"], 1)
                act.wait_ge(s["shifted"], b + NT + 1)
                A.activation(LP[:, :, :], LP[:, :, :], ACT.Exp).then_inc(s["probs_ready"], 1)
                for c in range(2):
                    act.wait_ge(s["cmbT_done"], b * 2 + c + 1)
                    if c == 0:
                        wait(act, s["cmb_stored"], b * 16)
                        act.wait_ge(s["rows_ready"], 1)
                    A.copy(cT8[0:E, c * C:(c + 1) * C], PS[0:E, 2 + c, :]).then_inc(s["cmbT_ready"], 1)

                for kind, g, u in ORDER:
                    if kind == "N":
                        for c in range(2):
                            act.wait_ge(s["nsT_done"], b * (2 * NG) + 2 * g + c + 1)
                            if c == 0:
                                wait(act, s["n_stored"], b * (16 * NG) + 16 * g)
                            A.copy(NR[:, c * C:(c + 1) * C], PS[0:3 * G4, 2, :]).then_inc(s["nr_ready"], 1)
                    elif kind == "S":
                        w = q_span(*steps[u])[1]
                        wait(act, s["pv_done"], b * (NG * NS_) + g * NS_ + max(0, u - 1))
                        for p in range(2):
                            act.wait_ge(s["s_scored"], b * (2 * NG * NS_) + 2 * (g * NS_ + u) + p + 1)
                            A.activation(PT[u % 2][:, 2 * p:2 * p + 2, 0:w], PS[:, 3 + 2 * p:5 + 2 * p, 0:w], ACT.Exp,
                                         scale=SCALE).then_inc(s["p_ready"], 1)
                    elif kind == "CE":
                        k = 2 * g + u
                        act.wait_ge(s["pv_done"], b * (NG * NS_) + g * NS_ + (4 if u == 0 else NS_))
                        wait(act, s["ctxT_done"], b * (2 * NG) + k)
                        A.copy(CA[:, :], PS[:, 7, :]).then_inc(s["c_evac"], 1)
                for j in range(TB):
                    act.wait_ge(s["woT_done"], b * TB + j + 1)
                    A.copy(cT[j % 2][:, :, :], PS[:, 2 + j % 2, 0:D].rearrange("p (k t) -> p k t", k=KD)).then_inc(s["wo_ready"], 1)

                def silu(v, par):
                    act.wait_ge(s["g_done"], b * 20 + v + 1)
                    wait(act, s["h_ready"], b * 20 + v - 1 if not isinstance(v, int) or v >= 2 else b * 20)
                    A.activation(SG[par], PS[:, 0:2, :], ACT.Silu).then_inc(s["silu_done"], 1)

                act.wait_ge(s["pv_done"], (b + 1) * (NG * NS_))
                for v in range(4):
                    silu(v, v % 2)
                with act.Fori(1, EA // 2) as k:
                    for v in range(4):
                        silu(k * 4 + v, v % 2)
                act.wait_ge(s["y_done"], b * 20 + 20)
                A.copy(YT[:, 0, :, :], PS[:, 4:6, :])
                A.copy(YT[:, 1, :, :], PS[:, 6:8, :]).then_inc(s["y_evac"], 1)

        @block.tensor
        def _(pe):
            M = nc.tensor
            pe.wait_ge(s["w_first"], 64)
            for m in range(KD):
                for k in range(KD):
                    M.matmul(PS[:, m, 0:NODE], wq_s[:, k, m * P:(m + 1) * P], rT_s[:, k, 0:NODE], start=k == 0, stop=k == KD - 1)
            for m in range(KD):
                for k in range(KD):
                    last = M.matmul(PS[:, 2 + m, 0:D], lT_s[:, k, m * P:(m + 1) * P], wwT_s[:, k, :], start=k == 0, stop=k == KD - 1)
            last.then_inc(s["fold_done"], 1)
            pe.wait_ge(s["const_done"], 1)
            pe.wait_ge(s["w_loaded"], 11 * 16)
            pe.wait_ge(s["fold_ready"], 1)

            def front(n, sl):
                pe.wait_ge(s["xn_ready"], n + 1)
                for k in range(KD):
                    last = M.transpose(PS[:, 4, k * P:(k + 1) * P], xn[sl][:, k * P:(k + 1) * P], ident[:, :])
                last.then_inc(s["xT_done"], 1)
                pe.wait_ge(s["xT_ready"], n + 1)
                if not (isinstance(n, int) and n < 2):
                    pe.wait_ge(s["gate_ready"], n - 1)
                for o, cols in ((0, C), (C, 3 * D)):
                    to = PS[:, (0 if o == 0 else 2) + sl, 0:cols - o]
                    M.matmul(to, ones[:, :], brow[:, o:cols], start=True, stop=False)
                    for k in range(KD):
                        M.matmul(to, xnT[sl][:, k, :], wqkv_s[:, k, o:cols], start=False, stop=k == KD - 1)
                for k in range(KD):
                    last = M.matmul(PS[:, 2 + sl, D:D + NODE], xnT[sl][:, k, :], rq_s[:, k, 0:NODE], start=k == 0, stop=k == KD - 1)
                last.then_inc(s["proj_done"], 1)

            def back(n, sl):
                pe.wait_ge(s["leaf_ready"], n + 1)
                pe.wait_ge(s["ctx_ready"], n + 1)
                c, lf = ctx0[sl].rearrange("p h d -> p (h d)"), leaf[sl].rearrange("p n c -> p (n c)")
                for k in range(KD):
                    M.transpose(PS[:, 5, k * P:(k + 1) * P], c[:, k * P:(k + 1) * P], ident[:, :])
                for k in range(KD):
                    last = M.transpose(PS[:, 5, (2 + k) * P:(3 + k) * P], lf[:, k * P:(k + 1) * P], ident[:, :])
                last.then_inc(s["backT_done"], 1)
                pe.wait_ge(s["back_ready"], n + 1)
                if not (isinstance(n, int) and n < 2):
                    pe.wait_ge(s["x2_done"], n - 1)
                to = PS[:, 6 + sl, 0:D]
                M.matmul(to, ones[:, :], brow_o[:, 0, :], start=True, stop=False)
                M.matmul(to, ones[:, :], brow_o[:, 1, :], start=False, stop=False)
                for k in range(KD):
                    M.matmul(to, clT[sl][:, k, :], wout_s[:, k, :], start=False, stop=False)
                for k in range(KD):
                    last = M.matmul(to, clT[sl][:, 2 + k, :], lw_s[:, k, :], start=False, stop=k == KD - 1)
                last.then_inc(s["out_done"], 1)

            front(0, 0)
            front(1, 1)
            back(0, 0)
            front(2, 0)
            back(1, 1)
            with pe.Fori(1, NT // 2 - 1) as k:
                front(k * 2 + 1, 1)
                back(k * 2, 0)
                front(k * 2 + 2, 0)
                back(k * 2 + 1, 1)
            front(NT - 1, 1)
            back(NT - 2, 0)
            back(NT - 1, 1)

            with pe.Fori(0, B) as b:
                for j in range(TB):
                    pe.wait_ge(s["ln_ready"], b * TB + j + 1)
                    if j >= 2:
                        pe.wait_ge(s["xbT_ready"], b * TB + (j - 1))
                    for k in range(KD):
                        last = M.transpose(PS[:, 4 + j % 2, k * P:(k + 1) * P], xn2[j % 2][:, k * P:(k + 1) * P], ident[:, :])
                    last.then_inc(s["lnT_done"], 1)
                pe.wait_ge(s["xbT_ready"], b * TB + TB)
                for u in range(8):
                    m, c = divmod(u, 2)
                    if u >= 4:
                        pe.wait_ge(s["kq_evac"], b * 8 + u - 3)
                    for k in range(KD):
                        last = M.matmul(PS[:, u % 4, :], wkqv_s[:, k, m * P:(m + 1) * P], xbT[:, k, c * C:(c + 1) * C],
                                        start=k == 0, stop=k == KD - 1)
                    last.then_inc(s["kq_done"], 1)
                for j in range(TB):
                    if j >= 2:
                        pe.wait_ge(s["v_evac"], b * TB + (j - 1))
                    to, tokens = PS[:, 4 + j % 2, 0:D], slice(j * P, (j + 1) * P)
                    M.matmul(to, ones[:, :], browv[:, :], start=True, stop=False)
                    for k in range(KD):
                        M.matmul(to, xbT[:, k, tokens], wkqv_s[:, k, 2 * D:3 * D], start=False, stop=k == KD - 1)
                    for k in range(KD):
                        last = M.matmul(PS[:, 4 + j % 2, D:D + E], xbT[:, k, tokens], rw_s[:, k, :], start=k == 0, stop=k == KD - 1)
                    last.then_inc(s["v_done"], 1)
                pe.wait_ge(s["kq_evac"], b * 8 + 8)
                pe.wait_ge(s["cmb_ready"], b + 1)
                for c in range(2):
                    for j in range(4):
                        last = M.transpose(PS[0:E, 2 + c, j * P:(j + 1) * P], CMB[:, 4 * c + j, :], ident[:, :])
                    last.then_inc(s["cmbT_done"], 1)
                pe.wait_ge(s["cmbT_ready"], b * 2 + 2)
                pe.wait_ge(s["v_evac"], b * TB + TB)

                for kind, g, u in ORDER:
                    Q, K = QS[g % 2], KS[g % 2]
                    if kind == "A":
                        hh, i, part = units[u]
                        w = min(C, (i + 1) * P - part * C)
                        if u == 0:
                            pe.wait_ge(stack[g % 2], (b * 2 + g // 2 + 1) * 192)
                        wait(pe, s["a_maxed"], b * (NG * NU) + g * NU + max(0, u - 1))
                        to = PS[:, u % 2, 0:w]
                        diag = (i + 1) * P - part * C <= C
                        last = M.matmul(to, Q[0:ROWS, hh, i * P:(i + 1) * P], K[0:ROWS, hh, part * C:part * C + w], start=True, stop=not diag)
                        if diag:
                            last = M.matmul(PS[:, u % 2, w - P:w], identb[:, :], mask_n[:, :], start=False, stop=True)
                        last.then_inc(s["a_scored"], 1)
                    elif kind == "N":
                        pe.wait_ge(s["ns_ready"], b * NG + g + 1)
                        cts = 2 * g if g == 0 else 2 * (g - 1) + 1
                        wait(pe, s["cn_done"], b * (2 * NG) + cts)
                        for c in range(2):
                            if c == 1:
                                pe.wait_ge(s["nr_ready"], b * (2 * NG) + 2 * g + 1)
                            for j in range(4):
                                last = M.transpose(PS[0:3 * G4, 2, j * P:(j + 1) * P], ns[:, 4 * c + j, :, :].rearrange("p a h -> p (a h)"), ident[:, :])
                            last.then_inc(s["nsT_done"], 1)
                    elif kind == "S":
                        qc, kt = steps[u]
                        q0, w = q_span(qc, kt)
                        if u == 0:
                            pe.wait_ge(neg[g % 2], (b * 2 + g // 2 + 1) * 16)
                        for p in range(2):
                            wait(pe, s["p_ready"], b * (2 * NG * NS_) + 2 * g * NS_ + (max(0, 2 * u + p - 1) if u else 0))
                            for hh in (2 * p, 2 * p + 1):
                                diag = q0 == kt * P
                                last = M.matmul(PS[:, 3 + hh, 0:w], K[0:ROWS_M, hh, kt * P:(kt + 1) * P], Q[0:ROWS_M, hh, q0:q0 + w],
                                                start=True, stop=not diag)
                                if diag:
                                    last = M.matmul(PS[:, 3 + hh, 0:P], identb[:, :], mask_t[:, :], start=False, stop=True)
                            last.then_inc(s["s_scored"], 1)
                    elif kind == "PV":
                        qc, kt = steps[u]
                        q0, w = q_span(qc, kt)
                        pe.wait_ge(s["p_ready"], b * (2 * NG * NS_) + 2 * (g * NS_ + u) + 2)
                        if kt == 0:
                            wait(pe, s["c_evac"], b * (2 * NG) + 2 * g + qc)
                        for hh in range(G4):
                            last = M.matmul(PS[32 * hh:32 * hh + 32, 7, q0 - qc * C:q0 - qc * C + w], vaug[:, kt, g * G4 + hh, :],
                                            PT[u % 2][:, hh, 0:w], start=kt == 0, stop=kt == 4 * qc + 3)
                        last.then_inc(s["pv_done"], 1)
                    elif kind == "CT":
                        k = 2 * g + u
                        pe.wait_ge(s["c_evac"], b * (2 * NG) + k + 1)
                        wait(pe, s["cn_done"], b * (2 * NG) + k)
                        pe.wait_ge(s["nr_ready"], b * (2 * NG) + 2 * min(NG, g + 1 + u))
                        for j in range(4):
                            last = M.transpose(PS[:, 2, j * P:(j + 1) * P], CA[:, j * P:(j + 1) * P], ident[:, :])
                        last.then_inc(s["ctxT_done"], 1)
                pe.wait_ge(s["cn_done"], b * (2 * NG) + 2 * NG)
                for j in range(TB):
                    if j >= 2:
                        pe.wait_ge(s["wo_added"], b * TB + (j - 1))
                    for k in range(KD):
                        last = M.transpose(PS[:, 2 + j % 2, k * P:(k + 1) * P], ctxN[:, j, k * P:(k + 1) * P], ident[:, :])
                    last.then_inc(s["woT_done"], 1)
                    pe.wait_ge(s["wo_ready"], b * TB + j + 1)
                    to = PS[:, 4 + j % 2, 0:D]
                    M.matmul(to, ones[:, :], brow1[:, :], start=True, stop=False)
                    for k in range(KD):
                        last = M.matmul(to, cT[j % 2][:, k, :], wo_s[:, k, :], start=False, stop=k == KD - 1)
                    last.then_inc(s["wo_done"], 1)
                pe.wait_ge(s["wo_added"], b * TB + TB)

                def gate_up(v, slot, k, c):
                    if c == 0:
                        pe.wait_ge(ew[slot], (b * 5 + k + 1) * 64)
                    for half_, free_, done in ((0, "silu_done", "g_done"), (1, "h_ready", "u_done")):
                        wait(pe, s[free_], b * 20 + v)
                        for f in range(2):
                            for kk in range(KD):
                                last = M.matmul(PS[:, 2 * half_ + f, :], w1[slot][:, kk, half_ * FF + f * P:half_ * FF + (f + 1) * P],
                                                xbT[:, kk, c * C:(c + 1) * C], start=kk == 0, stop=kk == KD - 1)
                        last.then_inc(s[done], 1)

                def down(v, slot, par, c, first=False):
                    pe.wait_ge(s["h_ready"], b * 20 + v + 1)
                    for m in range(KD):
                        for f in range(2):
                            last = M.matmul(PS[:, 4 + 2 * m + c, :], w2[slot][:, f, m * P:(m + 1) * P], HH[par][:, f, :],
                                            start=first and f == 0, stop=True, skip_group_check=True)
                    last.then_inc(s["y_done"], 1)

                gate_up(0, 0, 0, 0)
                for v in range(1, 4):
                    gate_up(v, v // 2, 0, v % 2)
                    down(v - 1, (v - 1) // 2, (v - 1) % 2, (v - 1) % 2, first=v - 1 < 2)
                with pe.Fori(1, EA // 2) as k:
                    for v in range(4):
                        gate_up(k * 4 + v, v // 2, k, v % 2)
                        down(k * 4 + (v - 1), ((v - 1) % 4) // 2, (v - 1) % 2, (v - 1) % 2)
                down(2 * EA - 1, 1, 1, 1)
                pe.wait_ge(s["y_evac"], b + 1)
                for j in range(TB):
                    if j >= 2:
                        pe.wait_ge(s["y_added"], b * TB + (j - 1))
                    for m in range(KD):
                        last = M.transpose(PS[:, j % 2, m * P:(m + 1) * P], YT[:, m, j // 4, (j % 4) * P:(j % 4 + 1) * P], ident[:, :])
                    last.then_inc(s["yT_done"], 1)


def kernel(**inputs):
    import numpy as np
    import concourse.bacc as bacc
    from concourse.bass_utils import run_bass_kernel_spmd

    a = {k: np.asarray(v) for k, v in inputs.items()}
    blocks = lambda w: np.stack([w[:, i * FF:(i + 1) * FF] for i in range(ES)])
    laid = {
        "x": a["L0_attn_x"].reshape(N, D),
        "w_qkv": a["L0_attn_W_qkv"], "b_qkv": a["L0_attn_b_qkv"],
        "w_out": a["L0_attn_W_out"], "b_out0": a["L0_attn_b_out"],
        "wq": a["L0_ffn_Wq"], "routersT": a["L0_ffn_routers"].T, "leafT": a["L0_ffn_leaf_values"].T,
        "woutT": a["L0_ffn_Wout_w"].T, "wout_b": a["L0_ffn_Wout_b"],
        "w_kqv": a["L1_attn_W_kqv"], "b_kqv": a["L1_attn_b_kqv"],
        "b_kq": a["L1_attn_b_kqv"][:2 * D].reshape(4, P).T,
        "w_o": a["L1_attn_W_o"], "b_o": a["L1_attn_b_o"], "router_w": a["L1_ffn_router_w"],
        "w_gate": np.concatenate([a["L1_ffn_gate_w"], blocks(a["L1_ffn_shared_gate_w"])]),
        "w_up": np.concatenate([a["L1_ffn_up_w"], blocks(a["L1_ffn_shared_up_w"])]),
        "w_down": np.concatenate([a["L1_ffn_down_w"], a["L1_ffn_shared_down_w"].reshape(ES, FF, D)]),
    }
    nc = bacc.Bacc("TRN2", target_bir_lowering=False, num_devices=1)
    laid = {k: np.ascontiguousarray(v) for k, v in laid.items()}
    aps = [nc.dram_tensor(f"in_{k}", v.shape, mybir.dt.from_np(v.dtype), kind="ExternalInput").ap() for k, v in laid.items()]
    out = nc.dram_tensor("out_0", (N, D), F32, kind="ExternalOutput").ap()
    build(nc, *aps, out)
    r = run_bass_kernel_spmd(nc, [{f"in_{k}": v for k, v in laid.items()}], core_ids=[0])
    return r.results[0]["out_0"].reshape(B, T, D)
```

```python
from contextlib import ExitStack

import concourse.bass as bass
from concourse import mybir

F32 = mybir.dt.float32
BF16 = mybir.dt.bfloat16
F32R = mybir.dt.float32r
ACT = mybir.ActivationFunctionType
ALU = mybir.AluOpType
AX = mybir.AxisListType

P = 128
B, T, D = 4, 1024, 256
N = B * T
NT = N // P
TB = T // P
KD = D // P
H, DK = 16, 16
NODE = 255
DEPTH = 8
E, ES = 8, 2
EA = E + ES
FF = 256
C = 512
NC_ = T // C
EPS = 1e-5
SCALE = 1.0 / DK ** 0.5
NEG = -1.0e30
LOWEST = -3.0e38
HP = 7
G4 = 4
NG = H // G4
PAIRS = [(0, 0), (0, 1), (1, 0), (1, 1), (0, 2), (2, 0)]
ROWS = len(PAIRS) * DK
ROWS_M = ROWS + 3


class Steps:

    def __init__(self, eng, sem):
        self.eng, self.sem, self.at, self.n, self.outer = eng, sem, 0, 0, []

    def did(self, instruction):
        instruction.then_inc(self.sem, 1)
        self.n += 1
        self.eng.wait_ge(self.sem, self.at + self.n)

    def enter(self, i, per):
        self.outer.append((self.at, self.n))
        self.at, self.n = self.at + self.n + i * per, 0

    def leave(self, count, per):
        assert self.n == per, (self.n, per)
        self.at, self.n = self.outer.pop()
        self.n += count * per


def spread(main, other):
    merged, k = [], 0
    for i, item in enumerate(main):
        merged.append(item)
        upto = len(other) * (i + 1) // len(main)
        merged += other[k:upto]
        k = upto
    return merged


steps = [(qc, kt) for qc in range(NC_) for kt in range(4 * (qc + 1))]
units = [(hh, i, part) for hh in range(G4) for i in range(TB) for part in range(1 + (i >= 4))]
NS_, NU = len(steps), len(units)
KQ_ORDER = [0, 2, 1, 3]
NV = NC_ * EA
NQ = 2 * NV


def attention_order():
    order = [("A", 0, u) for u in range(NU)] + [("N", 0, 0), ("R", 0, 0)]
    pending = None
    for g in range(NG):
        order.append(("S", g, 0))
        for t in range(NS_):
            if g + 1 < NG:
                per = NU // 8
                order += [("A", g + 1, u) for u in range(per * t, min(NU, per * t + per))]
                if t == 8:
                    order.append(("N", g + 1, 0))
            if t + 1 < NS_:
                order.append(("S", g, t + 1))
            order.append(("PV", g, t))
            if pending:
                order.append(pending)
                pending = None
            if t + 1 == NS_ or steps[t + 1][0] != steps[t][0]:
                order.append(("CE", g, steps[t][0]))
                pending = ("CT", g, steps[t][0])
    return order + [pending]


def tile_order():
    order = [(f"T{i}", 0) for i in range(4)]
    for j in range(TB):
        back, more = j > 0, j + 1 < TB
        order += [("K0", j - 1)] * back + [("H0", j)] + [("K1", j - 1)] * back + [("H1", j), ("H2", j)]
        order += [("T0", j + 1)] * more + [("H3", j)] + [("T1", j + 1)] * more + [("H4", j), ("H5", j)]
        order += [("T2", j + 1)] * more + [("H6", j), ("H7", j)] + [("T3", j + 1)] * more
        order += [("H8", j), ("H9", j), ("H10", j)]
    return order + [("K0", TB - 1), ("K1", TB - 1)]


def expert_order():
    order = []
    for v in range(NV + 1):
        for f in range(2):
            if v < NV:
                order += [("G", 2 * v + f), ("U", 2 * v + f)]
            q = 2 * v + f - 1
            if 0 <= q < NQ:
                order.append(("X", q))
            if v > 0:
                order.append(("D", 2 * (v - 1) + f))
    return order


ATTENTION, TILES, EXPERTS = attention_order(), tile_order(), expert_order()
BOTH = spread(EXPERTS, TILES)
USES = [e for e in TILES if e[0] in ("T1", "T2", "T3", "K0", "K1")]
TILE_USE = {e: n for n, e in enumerate(USES)}
LAST_READ = {"T1": "xlow_ready", "T2": "half_ready", "T3": "tanh_done", "K0": "clow_ready", "K1": "x2_done"}
OWN = [(HP, HP + (H - HP + 1) // 2), (HP + (H - HP + 1) // 2, H)]
SHARE = [(h, min(HP, h + 2)) for h in range(0, HP, 2)]


def q_span(qc, kt):
    first = max(qc * C, kt * P)
    return first, (qc + 1) * C - first


def build(nc, x, w_qkv, b_qkv, w_out, b_out0, wq, routersT, leafT, woutT, wout_b, w_kqv, b_kqv, b_kq, w_o,
          b_o, router_w, w_gate, w_up, w_down, out):
    ctx = ExitStack()
    with ctx:
        def sb(name, shape, dt=F32):
            return ctx.enter_context(nc.sbuf_tensor(name, shape, dt))

        xs = sb("xs", [P, NT, D])
        wqkv_r = sb("wqkv_r", [P, 2, KD, 3 * D], F32R)
        rq_r = sb("rq_r", [P, 2, KD, D], F32R)
        wout_r = sb("wout_r", [P, 2, KD, D], F32R)
        lw_r = sb("lw_r", [P, 2, KD, D], F32R)
        wkqv_r = sb("wkqv_r", [P, 2, KD, 3 * D], F32R)
        wo_r = sb("wo_r", [P, 2, KD, D], F32R)
        rw_r = sb("rw_r", [P, 2, KD, E], F32R)
        rw_s = sb("rw_s", [P, KD, E])
        bias_r = sb("bias_r", [2, 6 * D], F32R)
        BQKV, BOUT, BV, BO = 0, 3 * D, 4 * D, 5 * D
        ones_r = sb("ones_r", [2, P], F32R)
        bkq = sb("bkq", [P, 4])
        ident = sb("ident", [P, P])
        identb = sb("identb", [P, P], BF16)
        mask_n = sb("mask_n", [P, P], BF16)
        mask_t = sb("mask_t", [P, P], BF16)
        one = sb("one", [P, 1])
        pause = sb("pause", [P, 1])
        idle = sb("idle", [P, 1])
        half = sb("half", [P, TB])
        st = sb("st", [P, 2 * TB, 6])
        mv = sb("mv", [P, 2 * TB, 2])
        var = sb("var", [P, 2 * TB])
        rstd = sb("rstd", [P, 2 * TB])
        xbT = sb("xbT", [P, 2, KD, T], F32R)
        nmp = sb("nmp", [P, G4, TB, 2])
        nm = sb("nm", [P, TB, G4])
        nmr = sb("nmr", [P, TB, G4])
        nmb = sb("nmb", [P, TB, G4], BF16)
        ns = sb("ns", [P, TB, 3, G4])
        rc = sb("rc", [P, G4, G4])
        LG = sb("LG", [P, TB, E])
        LP = sb("LP", [P, TB, E])
        CMB = sb("CMB", [P, TB, E])
        lmax = sb("lmax", [P, TB])
        lsum = sb("lsum", [P, TB])
        top8 = sb("top8", [P, TB, 8])
        rep8 = sb("rep8", [P, TB, 8])
        xn2 = [sb(f"xn2_{i}", [P, D]) for i in range(2)]

        AREA = 26944
        base = nc.sbuf_base
        arena = sb("arena", [P, AREA])
        free, pieces = [0], []

        def take(shape, dt=F32, rows=P):
            words = 1
            for n in shape:
                words *= n
            if dt == BF16:
                words //= 2
            pieces.append(nc.alloc_sbuf_tensor_at(f"piece{len(pieces)}", [rows, *shape], dt, offset=base + 4 * free[0]))
            free[0] += (words + 7) // 8 * 8
            assert free[0] <= AREA, free[0]
            return pieces[-1][(slice(None),) * (1 + len(shape))]

        parts = [take([4, T], BF16) for _ in range(3)]
        QS = [take([G4, T], BF16) for _ in range(2)]
        KS = [take([G4, T], BF16) for _ in range(2)]
        pt_at = free[0]
        PT = [take([G4, C]) for _ in range(2)]
        vaug = take([TB, H, 32])
        ctxN = take([TB, D])
        CA = take([C])
        NR = take([T], BF16, rows=3 * G4)
        cT8 = take([T], rows=E)
        free[0] = pt_at
        XF = [take([C]) for _ in range(2)]
        RR = take([C])
        cT = [take([2, KD, P], F32R) for _ in range(2)]
        free[0] = 0
        ww = [take([2, KD, 3 * FF], F32R) for _ in range(2)]
        assert free[0] <= 3 * 4 * T // 2
        cb = [take([T]) for _ in range(2)]
        SG = [take([C]) for _ in range(2)]
        HS = [take([C]) for _ in range(2)]
        HF = [take([C]) for _ in range(2)]
        h_at = free[0]
        HR = [take([2, 2, C], F32R) for _ in range(2)]
        tiles_at = free[0]
        free[0] = h_at
        YT = take([KD, NC_, C])
        free[0] = tiles_at
        prod = take([H, H, DK])
        qkv = [take([H, 3, DK]) for _ in range(2)]
        gates = [take([D]) for _ in range(2)]
        xn = [take([D]) for _ in range(2)]
        xnT = [take([2, KD, P], F32R) for _ in range(2)]
        att = take([H, H])
        prob = take([H, H])
        mx = take([H])
        sums = take([H])
        ctx0 = [take([H, DK]) for _ in range(2)]
        tree = [take([2 ** l]) for l in range(1, DEPTH)]
        leaf = [take([D // 2, 2]) for _ in range(2)]
        clT = [take([2, 4, P], F32R) for _ in range(2)]
        free[0] = 0
        wq_s, rT_s, lT_s, wwT_s = (take([KD, D]) for _ in range(4))
        wqkv_s, wkqv_s = (take([KD, 3 * D]) for _ in range(2))
        wout_s, wo_s = (take([KD, D]) for _ in range(2))
        eraw = [take([KD, 3 * FF]) for _ in range(2)]
        ehl = [take([2, KD, 3 * FF], F32R) for _ in range(2)]
        assert free[0] <= tiles_at
        free[0] = tiles_at
        braw = take([7 * D], rows=1)
        blow = take([6 * D], F32R, rows=1)
        plain_ones = take([C], rows=ES)

        PS = ctx.enter_context(nc.psum_tensor("PS", [P, 8, C], F32))
        ACC, TILE = 3, 7

        scr_parts = nc.dram_tensor("scr_parts", (3, 4, P, T), BF16).ap()
        scr_neg = nc.dram_tensor("scr_neg", (3, G4, T), BF16).ap()
        scr_cmb = nc.dram_tensor("scr_cmb", (EA, T), F32).ap()
        scr_w = nc.dram_tensor("scr_w", (EA, P, 2, KD, 3 * FF), F32).ap()

        s = {name: ctx.enter_context(nc.semaphore(name)) for name in (
            "folds_loaded x_loaded others_loaded w_loaded const_done fold_done high_done low_done brow_loaded "
            "bsum_ready blow_ready bias_ready ones_stored consts_ready eraw0 eraw1 ehigh_done elow_done e_stored0 e_stored1 "
            "d_step p_step "
            "var_ready rstd_ready xn_ready xT_done xhigh_ready xlow_ready half_ready proj1_done "
            "proj2_done qkv_ready tanh_done gate_ready mulp_done part_reduced shifted probs_ready "
            "leaf_ready ctx_ready backT_done chigh_ready clow_ready out_done x2_done "
            "ln_ready lnT_done bhigh_ready blow2_ready kq_done kq_evac parts_ready "
            "parts_stored v_done v_evac lshifted lprobs_ready cmb_ready cmbT_done cmbT_ready "
            "cmb_stored stack0 stack1 neg0 neg1 a_scored a_maxed ns_ready nsT_done nr_ready n_stored "
            "s_scored p_ready pv_done c_evac ctxT_done cn_done woT_done wohigh_ready wolow_ready "
            "wo_done wo_added "
            "ew0 ew1 ec0 ec1 gu_done silu_done hs_ready hf_ready hhigh_ready hlow_ready y_done "
            "y_evac yT_done y_added stored").split()}
        stack, neg = [s["stack0"], s["stack1"]], [s["neg0"], s["neg1"]]
        eraw_loaded = [s["eraw0"], s["eraw1"]]
        e_stored = [s["e_stored0"], s["e_stored1"]]
        ew, ec = [s["ew0"], s["ew1"]], [s["ec0"], s["ec1"]]

        def W(eng, name, b, per, c):
            if c > 0:
                eng.wait_ge(s[name] if isinstance(name, str) else name, b * per + c)

        block = ctx.enter_context(nc.Block())

        @block.sync
        def _(sp):
            xv = x.rearrange("(n p) d -> p n d", p=P)
            wv = lambda w: w.rearrange("(k p) n -> p k n", p=P)
            row = lambda a: a.rearrange("(o n) -> o n", o=1)
            sp.dma_start(xs[:, 0:TB, :], xv[:, 0:TB, :]).then_inc(s["x_loaded"], 16)
            for dst, src in ((wq_s, wq), (rT_s, routersT), (lT_s, leafT), (wwT_s, woutT)):
                sp.dma_start(dst, wv(src)).then_inc(s["folds_loaded"], 16)
            for o, src in ((0, b_qkv), (3 * D, b_out0), (6 * D, wout_b), (5 * D, b_o)):
                sp.dma_start(braw[:, o:o + src.shape[0]], row(src)).then_inc(s["brow_loaded"], 16)
            sp.dma_start(braw[:, 4 * D:5 * D], row(b_kqv)[:, 2 * D:3 * D]).then_inc(s["brow_loaded"], 16)
            for dst, src in ((wqkv_s, w_qkv), (wout_s, w_out), (wkqv_s, w_kqv), (wo_s, w_o), (rw_s[:, :, :], router_w)):
                sp.dma_start(dst, wv(src)).then_inc(s["w_loaded"], 16)
            sp.dma_start(bkq[:, :], b_kq).then_inc(s["w_loaded"], 16)
            sp.wait_ge(s["consts_ready"], 1)
            for c in range(NC_):
                sp.dma_start(scr_cmb[E:EA, c * C:(c + 1) * C], plain_ones).then_inc(s["ones_stored"], 16)
            for e in range(EA + 1):
                if e < EA:
                    if e >= 2:
                        sp.wait_ge(s["elow_done"], e - 1)
                    for o, w in enumerate((w_gate, w_up, w_down)):
                        sp.dma_start(eraw[e % 2][:, :, o * FF:(o + 1) * FF], wv(w[e])).then_inc(eraw_loaded[e % 2], 16)
                if e == 1:
                    for i in range(1, B):
                        sp.dma_start(xs[:, i * TB:(i + 1) * TB, :], xv[:, i * TB:(i + 1) * TB, :]).then_inc(s["others_loaded"], 16)
                if e >= 1:
                    sp.wait_ge(s["elow_done"], e)
                    sp.dma_start(scr_w[e - 1], ehl[(e - 1) % 2].bitcast(F32)).then_inc(e_stored[(e - 1) % 2], 16)

            def attention(b):
                def store_parts(n):
                    W(sp, "parts_ready", b, 8, 4 * n + 4)
                    for p in range(3):
                        for blk in KQ_ORDER[2 * n:2 * n + 2]:
                            sp.dma_start(scr_parts[p, blk], parts[p][:, blk, :]).then_inc(s["parts_stored"], 16)

                def load_stack(g):
                    if g % 2 == 0:
                        W(sp, "parts_stored", b, 192, 96 * (g // 2) + 96)
                    W(sp, "pv_done", b, NG * NS_, NS_ * (g - 1))
                    for dst, base, side in ((KS, 0, 1), (QS, 2, 0)):
                        for r, pair in enumerate(PAIRS):
                            p0 = (g % 2) * G4 * DK
                            src = scr_parts[pair[side], base + g // 2, p0:p0 + G4 * DK, :]
                            sp.dma_start(dst[g % 2][r * DK:(r + 1) * DK, :, :],
                                         src.rearrange("(h d) t -> d h t", d=DK)).then_inc(stack[g % 2], 16)

                def load_neg(g):
                    W(sp, "nr_ready", b, 2 * NG, 2 * g + 2)
                    sp.dma_start(scr_neg.rearrange("p h t -> (p h) t"), NR).then_inc(s["n_stored"], 16)
                    W(sp, "n_stored", b, 16 * NG, 16 * (g + 1))
                    sp.dma_start(QS[g % 2][ROWS:ROWS_M, :, :], scr_neg).then_inc(neg[g % 2], 16)

                store_parts(0)
                load_stack(0)
                load_stack(1)
                store_parts(1)
                load_neg(0)
                W(sp, "cmbT_ready", b, 2, 2)
                sp.dma_start(scr_cmb[0:E, :], cT8).then_inc(s["cmb_stored"], 16)
                load_neg(1)
                load_stack(2)
                load_neg(2)
                load_stack(3)
                load_neg(3)

            def load_cb(e, slot):
                src = scr_cmb[bass.ds(e, 1), :].partition_broadcast(P).rearrange("p o t -> p (o t)")
                sp.dma_start(cb[slot], src).then_inc(ec[slot], 16)

            def experts(b):
                W(sp, "pv_done", b, NG * NS_, NG * NS_)
                W(sp, "cmb_stored", b, 16, 16)
                for e in range(2):
                    load_cb(e, e)
                for e in range(2, EA):
                    W(sp, "hf_ready", b, NQ, 4 * (e - 1))
                    load_cb(e, e % 2)
                W(sp, "y_added", b, TB, TB)
                ov = out.rearrange("(b n p) d -> b p n d", p=P, b=B)
                sp.dma_start(ov[bass.ds(b, 1), :, :, :].rearrange("o p n d -> p (o n) d"),
                             xs[:, bass.ds(b * TB, TB), :]).then_inc(s["stored"], 16)

            for slot in range(2):
                sp.wait_ge(e_stored[slot], 16 * (EA // 2))
            with sp.Fori(0, B - 1) as b:
                attention(b)
                experts(b)
            attention(B - 1)
            experts(B - 1)
            sp.wait_ge(s["stored"], B * 16)

        @block.gpsimd
        def _(pool):
            G = nc.gpsimd
            step = Steps(pool, s["p_step"])
            step.did(G.memset(ident[:, :], 0.0))
            step.did(G.affine_select(out=ident[:, :], in_=ident[:, :], compare_op=ALU.not_equal, fill=1.0,
                                     base=0, pattern=[[-1, P]], channel_multiplier=1))
            step.did(G.memset(plain_ones, 1.0))
            G.tensor_scalar(ones_r[:, :], plain_ones[:, 0:P], 1.0, None, ALU.mult).then_inc(s["consts_ready"], 1)
            G.memset(one[:, :], 1.0)
            step.did(G.memset(half[:, :], -0.5))
            step.did(G.memset(mask_n[:, :], 0.0))
            step.did(G.memset(mask_t[:, :], 0.0))
            step.did(G.affine_select(out=mask_n[:, :], in_=mask_n[:, :], compare_op=ALU.is_ge, fill=NEG,
                                     base=0, pattern=[[-1, P]], channel_multiplier=1))
            step.did(G.affine_select(out=mask_t[:, :], in_=mask_t[:, :], compare_op=ALU.is_ge, fill=NEG,
                                     base=0, pattern=[[1, P]], channel_multiplier=-1))
            G.tensor_scalar(identb[:, :], ident[:, :], 1.0, None, ALU.mult).then_inc(s["const_done"], 1)

            def power(n, sl):
                pool.wait_ge(s["var_ready"], n)
                lo = sl * TB
                G.tensor_tensor(rstd[:, lo:lo + TB], var[:, lo:lo + TB], half[:, :], ALU.pow).then_inc(s["rstd_ready"], 1)

            def tile(kind, j, bt):
                if kind[0] != "H":
                    return
                h, sl, g = int(kind[1:]), j % 2, gates[j % 2]
                q, k, v = (qkv[sl][:, :, i, :] for i in range(3))
                if h < len(SHARE):
                    a, z = SHARE[h]
                    if h == 0:
                        W(pool, "qkv_ready", bt, TB, j + 1)
                        W(pool, "part_reduced", bt, 2 * TB, 2 * j)
                    i = G.tensor_tensor(prod[:, a:z, :, :], q[:, a:z, :].unsqueeze(2).to_broadcast([P, z - a, H, DK]),
                                        k.unsqueeze(1).to_broadcast([P, z - a, H, DK]), ALU.mult)
                    if h == len(SHARE) - 1:
                        i.then_inc(s["mulp_done"], 1)
                levels = {4: range(0, 5), 5: range(5, 6), 9: range(6, 7), 10: range(7, 8)}.get(h, ())
                for l in levels:
                    m = 2 ** l
                    if l == 0:
                        W(pool, "gate_ready", bt, TB, j + 1)
                        G.tensor_tensor(tree[0][:, 0:1], one[:, :], g[:, 0:1], ALU.subtract)
                        step.did(G.tensor_tensor(tree[0][:, 1:2], one[:, :], g[:, 0:1], ALU.mult))
                        continue
                    if l == DEPTH - 1:
                        W(pool, "backT_done", bt, TB, j - 1)
                    to = leaf[sl] if l == DEPTH - 1 else tree[l].rearrange("p (n c) -> p n c", c=2)
                    step.did(G.tensor_tensor(to[:, :, 1], tree[l - 1], g[:, m - 1:2 * m - 1], ALU.mult))
                    i = G.tensor_tensor(to[:, :, 0], tree[l - 1], to[:, :, 1], ALU.subtract)
                    if l < DEPTH - 1:
                        step.did(i)
                    else:
                        i.then_inc(s["leaf_ready"], 1)
                if 6 <= h < 6 + len(SHARE):
                    a, z = SHARE[h - 6]
                    if h == 6:
                        W(pool, "probs_ready", bt, TB, j + 1)
                        W(pool, "part_reduced", bt, 2 * TB, 2 * j + 1)
                    i = G.tensor_tensor(prod[:, a:z, :, :], prob[:, a:z, :].unsqueeze(2).to_broadcast([P, z - a, DK, H]),
                                        v.rearrange("p g d -> p d g").unsqueeze(1).to_broadcast([P, z - a, DK, H]), ALU.mult)
                    if h - 6 == len(SHARE) - 1:
                        i.then_inc(s["mulp_done"], 1)

            def expert(kind, q, b):
                if kind != "U":
                    return
                v = q // 2
                e, c = divmod(v, 2)
                if q % 4 == 2 and 2 <= e + 1 < EA:
                    W(pool, "y_done", b, NQ, 4 * e)
                    rest()
                    load_weights(e + 1)
                if v % 2 == 0 and q % 2 == 0:
                    W(pool, ec[e % 2], b, 16 * 5, 16 * (e // 2 + 1))
                W(pool, "hs_ready", b, NQ, q + 1)
                W(pool, "hlow_ready", b, NQ, q - 1)
                G.tensor_tensor(HF[q % 2], HS[q % 2], cb[e % 2][:, c * C:(c + 1) * C], ALU.mult).then_inc(s["hf_ready"], 1)

            def rest():
                G.tensor_tensor(idle[:, :], one[:, :], one[:, :], ALU.mult)

            def load_weights(e):
                G.dma_start(ww[e % 2], scr_w[e]).then_inc(ew[e % 2], 16)

            def both(b, events):
                for kind, n in events:
                    if kind[0] in "THK":
                        tile(kind, n, b + 1)
                    else:
                        expert(kind, n, b)

            def start(b):
                W(pool, "parts_stored", b, 192, 192)
                rest()
                for e in range(2):
                    load_weights(e)

            pool.wait_ge(s["blow_ready"], 1)
            G.dma_start(bias_r[1:2, :], blow.bitcast(F32)).then_inc(s["bias_ready"], 16)
            power(1, 0)
            for kind, j in TILES:
                tile(kind, j, 0)
            per = TB * (1 + 2 * (DEPTH - 2) + 1)
            for slot in range(2):
                pool.wait_ge(e_stored[slot], 16 * (EA // 2))
            with pool.Fori(0, B - 1) as b:
                step.enter(b, per)
                power(b * 2 + 2, 1)
                power(b * 2 + 3, 0)
                start(b)
                both(b, BOTH)
                step.leave(B - 1, per)
            power(2 * B, 1)
            start(B - 1)
            both(B - 1, EXPERTS)

        @block.vector
        def _(dve):
            V = nc.vector
            step = Steps(dve, s["d_step"])

            def low(to, whole, high):
                return V.tensor_tensor(to, whole, high.bitcast(F32), ALU.subtract)

            def norm_stats(tile0, sl):
                lo = sl * TB
                for j in range(TB):
                    i = V.bn_stats(st[:, lo + j, :], xs[:, tile0 + j, :])
                step.did(i)
                V.memset(pause[:, :], 0.0)
                for j in range(TB):
                    i = V.bn_aggr(mv[:, lo + j, :], st[:, lo + j, :])
                step.did(i)
                V.tensor_scalar(var[:, lo:lo + TB], mv[:, lo:lo + TB, 1], EPS, None, ALU.add).then_inc(s["var_ready"], 1)

            V.memset(nmp[:, :, :, :], LOWEST)
            V.memset(rep8[:, :, :], -1.0)
            dve.wait_ge(s["x_loaded"], 16)
            norm_stats(0, 0)
            dve.wait_ge(s["brow_loaded"], 5 * 16)
            V.tensor_tensor(braw[:, 3 * D:4 * D], braw[:, 3 * D:4 * D], braw[:, 6 * D:7 * D], ALU.add).then_inc(s["bsum_ready"], 1)
            dve.wait_ge(s["high_done"], 1)
            low(blow, braw[:, 0:6 * D], bias_r[0:1, :]).then_inc(s["blow_ready"], 1)
            for n, (r, w) in enumerate(((wqkv_r, wqkv_s), (wout_r, wout_s), (wkqv_r, wkqv_s), (wo_r, wo_s), (rw_r, rw_s[:, :, :]))):
                dve.wait_ge(s["high_done"], n + 2)
                low(r[:, 1, :, :], w, r[:, 0, :, :])
            dve.wait_ge(s["high_done"], 7)
            low(rq_r[:, 1, :, :], PS[:, 0:2, 0:D], rq_r[:, 0, :, :])
            low(lw_r[:, 1, :, :], PS[:, 2:4, 0:D], lw_r[:, 0, :, :]).then_inc(s["low_done"], 1)

            def tile(kind, j, bt):
                sl = j % 2
                q, k, v = (qkv[sl][:, :, i, :] for i in range(3))

                def scores(a, z):
                    return V.tensor_tensor(prod[:, a:z, :, :], q[:, a:z, :].unsqueeze(2).to_broadcast([P, z - a, H, DK]),
                                           k.unsqueeze(1).to_broadcast([P, z - a, H, DK]), ALU.mult)

                def values(a, z):
                    return V.tensor_tensor(prod[:, a:z, :, :], prob[:, a:z, :].unsqueeze(2).to_broadcast([P, z - a, DK, H]),
                                           v.rearrange("p g d -> p d g").unsqueeze(1).to_broadcast([P, z - a, DK, H]), ALU.mult)

                def summed(a, z):
                    return V.tensor_reduce(att[:, a:z, :], prod[:, a:z, :, :], AX.X, ALU.add)

                if kind == "T0":
                    W(dve, "xT_done", bt, TB, j - 1)
                    V.tensor_scalar(xn[sl], xs[:, bt * TB + j, :], mv[:, j, 0:1], rstd[:, j:j + 1],
                                    ALU.subtract, ALU.mult).then_inc(s["xn_ready"], 1)
                elif kind == "T1":
                    W(dve, "xhigh_ready", bt, TB, j + 1)
                    i = low(xnT[sl][:, 1, :, :], PS[:, TILE, 0:D].rearrange("p (k t) -> p k t", k=KD), xnT[sl][:, 0, :, :])
                    i.then_inc(s["xlow_ready"], 1)
                elif kind == "H0":
                    W(dve, "qkv_ready", bt, TB, j + 1)
                    step.did(scores(*OWN[0]))
                elif kind == "H1":
                    step.did(scores(*OWN[1]))
                elif kind == "H2":
                    summed(*OWN[0])
                elif kind == "H3":
                    summed(*OWN[1])
                elif kind in ("H4", "H10"):
                    n = 2 * j + 1 + (kind == "H10")
                    W(dve, "mulp_done", bt, 2 * TB, n)
                    summed(0, HP).then_inc(s["part_reduced"], 1)
                    W(dve, "part_reduced", bt, 2 * TB, n)
                    if kind == "H10":
                        W(dve, "backT_done", bt, TB, j - 1)
                        V.tensor_tensor(ctx0[sl], att, mx.unsqueeze(2).to_broadcast([P, H, DK]), ALU.mult).then_inc(s["ctx_ready"], 1)
                elif kind == "H5":
                    step.did(V.tensor_reduce(mx, att, AX.X, ALU.max))
                    V.tensor_tensor(att, att, mx.unsqueeze(2).to_broadcast([P, H, H]), ALU.subtract).then_inc(s["shifted"], 1)
                elif kind == "H6":
                    W(dve, "probs_ready", bt, TB, j + 1)
                    step.did(V.tensor_reduce(sums, prob, AX.X, ALU.add))
                    V.reciprocal(mx, sums)
                    step.did(values(*OWN[0]))
                elif kind == "H7":
                    step.did(values(*OWN[1]))
                elif kind == "H8":
                    summed(*OWN[0])
                elif kind == "H9":
                    summed(*OWN[1])
                elif kind == "K0":
                    W(dve, "chigh_ready", bt, TB, j + 1)
                    i = low(clT[sl][:, 1, :, :], PS[:, TILE, :].rearrange("p (k t) -> p k t", k=4), clT[sl][:, 0, :, :])
                    i.then_inc(s["clow_ready"], 1)
                elif kind == "K1":
                    W(dve, "out_done", bt, TB, j + 1)
                    V.tensor_tensor(xs[:, bt * TB + j, :], PS[:, TILE, 0:D], xs[:, bt * TB + j, :], ALU.add).then_inc(s["x2_done"], 1)

            def expert(kind, q, b):
                if kind == "U":
                    W(dve, "silu_done", b, NQ, q + 1)
                    W(dve, "gu_done", b, 2 * NQ, 2 * q + 2)
                    W(dve, "hf_ready", b, NQ, q - 1)
                    V.tensor_tensor(HS[q % 2], SG[q % 2], PS[:, (2 * q + 1) % 3, :], ALU.mult).then_inc(s["hs_ready"], 1)
                elif kind == "X":
                    W(dve, "hhigh_ready", b, NQ, q + 1)
                    v, f = divmod(q, 2)
                    low(HR[v % 2][:, 1, f, :], HF[q % 2], HR[v % 2][:, 0, f, :]).then_inc(s["hlow_ready"], 1)

            def both(b, events):
                for kind, n in events:
                    if kind[0] in "THK":
                        tile(kind, n, b + 1)
                    else:
                        expert(kind, n, b)
                for j in range(TB):
                    W(dve, "yT_done", b, TB, j + 1)
                    V.tensor_tensor(xs[:, b * TB + j, :], PS[:, j % 2, 0:D], xs[:, b * TB + j, :], ALU.add).then_inc(s["y_added"], 1)

            def attention(b, more):
                dve.wait_ge(s["x2_done"], b * TB + TB)
                norm_stats(b * TB, 1)
                if more:
                    norm_stats((b + 1) * TB, 0)
                V.memset(vaug[:, :, :, DK:32], 1.0)
                for sl in range(2):
                    V.memset(KS[sl][ROWS:ROWS_M, :, :], 1.0)
                dve.wait_ge(s["rstd_ready"], b * 2 + 2)
                for j in range(TB):
                    W(dve, "lnT_done", b, TB, j - 1)
                    V.tensor_scalar(xn2[j % 2][:, :], xs[:, b * TB + j, :], mv[:, TB + j, 0:1], rstd[:, TB + j:TB + j + 1],
                                    ALU.subtract, ALU.mult).then_inc(s["ln_ready"], 1)
                    if j >= 1:
                        low_xb(b, j - 1)
                low_xb(b, TB - 1)
                for u in range(8):
                    blk, c = KQ_ORDER[u // 2], u % 2
                    to = [a[:, blk, c * C:(c + 1) * C] for a in parts]
                    W(dve, "kq_evac", b, 8, u + 1)
                    step.did(V.tensor_copy(to[0], XF[u % 2]))
                    step.did(V.tensor_tensor(RR, XF[u % 2], to[0], ALU.subtract))
                    step.did(V.tensor_copy(to[1], RR))
                    V.tensor_tensor(to[2], RR, to[1], ALU.subtract).then_inc(s["parts_ready"], 1)
                    if u < 7:
                        W(dve, "parts_ready", b, 8, u + 1)

                for kind, g, u in ATTENTION:
                    if kind == "A":
                        hh, i, part = units[u]
                        w = min(C, (i + 1) * P - part * C)
                        W(dve, "a_scored", b, NG * NU, g * NU + u + 1)
                        V.tensor_reduce(nmp[:, hh, i, part:part + 1], PS[:, u % 2, 0:w], AX.X, ALU.max).then_inc(s["a_maxed"], 1)
                    elif kind == "N":
                        W(dve, "a_maxed", b, NG * NU, (g + 1) * NU)
                        W(dve, "nsT_done", b, 2 * NG, 2 * g)
                        step.did(V.tensor_reduce(nm[:, :, :].rearrange("p i h -> p h i"), nmp[:, :, :, :], AX.X, ALU.max))
                        step.did(V.tensor_scalar(nm[:, :, :], nm[:, :, :], -1.0, None, ALU.mult))
                        step.did(V.tensor_copy(nmb[:, :, :], nm[:, :, :]))
                        V.tensor_copy(ns[:, :, 0, :], nmb[:, :, :])
                        step.did(V.tensor_tensor(nmr[:, :, :], nm[:, :, :], nmb[:, :, :], ALU.subtract))
                        step.did(V.tensor_copy(nmb[:, :, :], nmr[:, :, :]))
                        V.tensor_copy(ns[:, :, 1, :], nmb[:, :, :])
                        V.tensor_tensor(ns[:, :, 2, :], nmr[:, :, :], nmb[:, :, :], ALU.subtract).then_inc(s["ns_ready"], 1)
                    elif kind == "R":
                        W(dve, "v_evac", b, TB, TB)
                        step.did(V.tensor_reduce(lmax[:, :], LG[:, :, :], AX.X, ALU.max))
                        V.tensor_tensor(LP[:, :, :], LG[:, :, :], lmax[:, :].unsqueeze(2).to_broadcast([P, TB, E]),
                                        ALU.subtract).then_inc(s["lshifted"], 1)
                        W(dve, "lprobs_ready", b, 1, 1)
                        step.did(V.tensor_reduce(lsum[:, :], LP[:, :, :], AX.X, ALU.add))
                        step.did(V.reciprocal(lmax[:, :], lsum[:, :]))
                        step.did(V.tensor_tensor(LP[:, :, :], LP[:, :, :], lmax[:, :].unsqueeze(2).to_broadcast([P, TB, E]), ALU.mult))
                        V.memset(pause[:, :], 0.0)
                        for j in range(TB):
                            i = V.max(top8[:, j, :], LP[:, j, :])
                        step.did(i)
                        step.did(V.tensor_copy(rep8[:, :, 0:2], top8[:, :, 0:2]))
                        V.memset(pause[:, :], 0.0)
                        for j in range(TB):
                            i = V.match_replace(out=CMB[:, j, :], in_to_replace=rep8[:, j, :], in_values=LP[:, j, :], imm_value=0.0)
                        step.did(i)
                        V.tensor_tensor(CMB[:, :, :], LP[:, :, :], CMB[:, :, :], ALU.subtract).then_inc(s["cmb_ready"], 1)
                    elif kind == "CT":
                        k = 2 * g + u
                        W(dve, "ctxT_done", b, 2 * NG, k + 1)
                        got = PS[:, 2, :].rearrange("p (q h e) -> p q h e", q=4, h=G4)
                        step.did(V.reciprocal(rc[:, :, :], got[:, :, :, DK]))
                        V.tensor_tensor(ctxN[:, 4 * u:4 * u + 4, g * G4 * DK:(g + 1) * G4 * DK].rearrange("p q (h d) -> p q h d", d=DK),
                                        got[:, :, :, 0:DK], rc[:, :, :].unsqueeze(3).to_broadcast([P, 4, G4, DK]),
                                        ALU.mult).then_inc(s["cn_done"], 1)
                for j in range(TB):
                    W(dve, "wohigh_ready", b, TB, j + 1)
                    low(cT[j % 2][:, 1, :, :], PS[:, 2 + j % 2, 0:D].rearrange("p (k t) -> p k t", k=KD),
                        cT[j % 2][:, 0, :, :]).then_inc(s["wolow_ready"], 1)
                    if j >= 1:
                        wo_add(b, j - 1)
                wo_add(b, TB - 1)

            def low_xb(b, j):
                W(dve, "bhigh_ready", b, TB, j + 1)
                t = slice(j * P, (j + 1) * P)
                low(xbT[:, 1, :, t], PS[:, 4 + j % 2, 0:D].rearrange("p (k t) -> p k t", k=KD), xbT[:, 0, :, t]).then_inc(s["blow2_ready"], 1)

            def wo_add(b, j):
                W(dve, "wo_done", b, TB, j + 1)
                V.tensor_tensor(xs[:, b * TB + j, :], PS[:, 4 + j % 2, 0:D], xs[:, b * TB + j, :], ALU.add).then_inc(s["wo_added"], 1)

            dve.wait_ge(s["rstd_ready"], 1)
            marks = [i for i, e in enumerate(TILES) if e[0] in ("H1", "H8")][:EA]
            for i, (kind, j) in enumerate(TILES):
                tile(kind, j, 0)
                if i in marks:
                    e = marks.index(i)
                    dve.wait_ge(s["ehigh_done"], e + 1)
                    low(ehl[e % 2][:, 1, :, :], eraw[e % 2], ehl[e % 2][:, 0, :, :]).then_inc(s["elow_done"], 1)
            dve.wait_ge(s["others_loaded"], 16 * (B - 1))
            for slot in range(2):
                dve.wait_ge(e_stored[slot], 16 * (EA // 2))
            per = 4 + 8 * 3 + NG * 5 + 7 + 2 * NG + 6 * TB
            with dve.Fori(0, B - 1) as b:
                step.enter(b, per)
                attention(b, True)
                dve.wait_ge(s["rstd_ready"], b * 2 + 3)
                both(b, BOTH)
                step.leave(B - 1, per)
            attention(B - 1, False)
            both(B - 1, EXPERTS)

        @block.scalar
        def _(act):
            A = nc.scalar

            def tile(kind, j, bt):
                sl = j % 2
                if kind == "T1":
                    W(act, "xT_done", bt, TB, j + 1)
                    W(act, "proj2_done", bt, TB, j - 1)
                    A.copy(xnT[sl][:, 0, :, :], PS[:, TILE, 0:D].rearrange("p (k t) -> p k t", k=KD)).then_inc(s["xhigh_ready"], 1)
                elif kind == "T2":
                    W(act, "proj1_done", bt, TB, j + 1)
                    W(act, "ctx_ready", bt, TB, j - 1)
                    W(act, "mulp_done", bt, 2 * TB, 2 * j - 2)
                    t = qkv[sl].rearrange("p h c d -> p (h c d)")
                    A.copy(t[:, 0:C], PS[:, TILE, :]).then_inc(s["half_ready"], 1)
                elif kind == "T3":
                    W(act, "proj2_done", bt, TB, j + 1)
                    t = qkv[sl].rearrange("p h c d -> p (h c d)")
                    A.copy(t[:, C:3 * D], PS[:, TILE, 0:3 * D - C]).then_inc(s["qkv_ready"], 1)
                    W(act, "leaf_ready", bt, TB, j - 1)
                    A.activation(gates[sl][:, 0:NODE], PS[:, TILE, D:D + NODE], ACT.Tanh, scale=0.5).then_inc(s["tanh_done"], 1)
                    W(act, "tanh_done", bt, TB, j + 1)
                    A.activation(gates[sl][:, 0:NODE], gates[sl][:, 0:NODE], ACT.Copy, scale=0.5, bias=0.5).then_inc(s["gate_ready"], 1)
                elif kind == "H5":
                    W(act, "shifted", bt, TB, j + 1)
                    W(act, "ctx_ready", bt, TB, j)
                    A.activation(prob, att, ACT.Exp, scale=SCALE).then_inc(s["probs_ready"], 1)
                elif kind == "K0":
                    W(act, "backT_done", bt, TB, j + 1)
                    W(act, "out_done", bt, TB, j - 1)
                    A.copy(clT[sl][:, 0, :, :], PS[:, TILE, :].rearrange("p (k t) -> p k t", k=4)).then_inc(s["chigh_ready"], 1)

            def expert(kind, q, b):
                v, f = divmod(q, 2)
                if kind == "G":
                    W(act, "gu_done", b, 2 * NQ, 2 * q + 1)
                    W(act, "hs_ready", b, NQ, q - 1)
                    A.activation(SG[q % 2], PS[:, (2 * q) % 3, :], ACT.Silu).then_inc(s["silu_done"], 1)
                elif kind == "X":
                    W(act, "hf_ready", b, NQ, q + 1)
                    W(act, "y_done", b, NQ, 2 * (v - 1))
                    A.copy(HR[v % 2][:, 0, f, :], HF[q % 2]).then_inc(s["hhigh_ready"], 1)

            def both(b, events):
                for kind, n in events:
                    if kind[0] in "THK":
                        tile(kind, n, b + 1)
                    else:
                        expert(kind, n, b)
                W(act, "y_done", b, NQ, NQ)
                A.copy(YT[:, 0, :, :], PS[:, ACC:ACC + 2, :])
                A.copy(YT[:, 1, :, :], PS[:, ACC + 2:ACC + 4, :]).then_inc(s["y_evac"], 1)

            def attention(b):
                for j in range(TB):
                    W(act, "lnT_done", b, TB, j + 1)
                    A.copy(xbT[:, 0, :, j * P:(j + 1) * P], PS[:, 4 + j % 2, 0:D].rearrange("p (k t) -> p k t", k=KD)).then_inc(s["bhigh_ready"], 1)
                for u in range(8):
                    W(act, "kq_done", b, 8, u + 1)
                    W(act, "parts_ready", b, 8, u - 1)
                    blk = KQ_ORDER[u // 2]
                    A.activation(XF[u % 2], PS[:, u % 4, :], ACT.Identity, bias=bkq[:, blk:blk + 1]).then_inc(s["kq_evac"], 1)
                for j in range(TB):
                    W(act, "v_done", b, TB, j + 1)
                    A.copy(vaug[:, j, :, 0:DK], PS[:, 4 + j % 2, 0:D].rearrange("p (h d) -> p h d", d=DK))
                    A.copy(LG[:, j, :], PS[:, 4 + j % 2, D:D + E]).then_inc(s["v_evac"], 1)
                for kind, g, u in ATTENTION:
                    if kind == "N":
                        for c in range(2):
                            W(act, "nsT_done", b, 2 * NG, 2 * g + c + 1)
                            if c == 0:
                                W(act, "n_stored", b, 16 * NG, 16 * g)
                            A.copy(NR[:, c * C:(c + 1) * C], PS[0:3 * G4, 2, :]).then_inc(s["nr_ready"], 1)
                    elif kind == "R":
                        W(act, "lshifted", b, 1, 1)
                        A.activation(LP[:, :, :], LP[:, :, :], ACT.Exp).then_inc(s["lprobs_ready"], 1)
                        for c in range(2):
                            W(act, "cmbT_done", b, 2, c + 1)
                            A.copy(cT8[:, c * C:(c + 1) * C], PS[0:E, 2, :]).then_inc(s["cmbT_ready"], 1)
                    elif kind == "S":
                        w = q_span(*steps[u])[1]
                        W(act, "pv_done", b, NG * NS_, g * NS_ + u - 1)
                        for p in range(2):
                            W(act, "s_scored", b, 2 * NG * NS_, 2 * (g * NS_ + u) + p + 1)
                            A.activation(PT[u % 2][:, 2 * p:2 * p + 2, 0:w], PS[:, 3 + 2 * p:5 + 2 * p, 0:w], ACT.Exp,
                                         scale=SCALE).then_inc(s["p_ready"], 1)
                    elif kind == "CE":
                        k = 2 * g + u
                        W(act, "pv_done", b, NG * NS_, g * NS_ + (4 if u == 0 else NS_))
                        W(act, "ctxT_done", b, 2 * NG, k)
                        A.copy(CA, PS[:, 7, :]).then_inc(s["c_evac"], 1)
                for j in range(TB):
                    W(act, "woT_done", b, TB, j + 1)
                    W(act, "wo_done", b, TB, j - 1)
                    A.copy(cT[j % 2][:, 0, :, :], PS[:, 2 + j % 2, 0:D].rearrange("p (k t) -> p k t", k=KD)).then_inc(s["wohigh_ready"], 1)

            act.wait_ge(s["bsum_ready"], 1)
            A.copy(bias_r[0:1, :], braw[:, 0:6 * D]).then_inc(s["high_done"], 1)
            act.wait_ge(s["w_loaded"], 6 * 16)
            for r, w in ((wqkv_r, wqkv_s), (wout_r, wout_s), (wkqv_r, wkqv_s), (wo_r, wo_s), (rw_r, rw_s[:, :, :])):
                A.copy(r[:, 0, :, :], w).then_inc(s["high_done"], 1)
            act.wait_ge(s["fold_done"], 1)
            A.copy(rq_r[:, 0, :, :], PS[:, 0:2, 0:D])
            A.copy(lw_r[:, 0, :, :], PS[:, 2:4, 0:D]).then_inc(s["high_done"], 1)
            marks = [i for i, e in enumerate(TILES) if e[0] in ("H0", "H7")][:EA]
            for i, (kind, j) in enumerate(TILES):
                tile(kind, j, 0)
                if i in marks:
                    e = marks.index(i)
                    act.wait_ge(eraw_loaded[e % 2], 48 * (e // 2 + 1))
                    if e >= 2:
                        act.wait_ge(e_stored[e % 2], 16 * (e // 2))
                    A.copy(ehl[e % 2][:, 0, :, :], eraw[e % 2]).then_inc(s["ehigh_done"], 1)
            for slot in range(2):
                act.wait_ge(e_stored[slot], 16 * (EA // 2))
            with act.Fori(0, B - 1) as b:
                attention(b)
                both(b, BOTH)
            attention(B - 1)
            both(B - 1, EXPERTS)

        @block.tensor
        def _(pe):
            M = nc.tensor

            def three(to, left, right, start, stop=True, skip=False):
                n = 0
                for k in range(KD):
                    for a, z in ((0, 0), (0, 1), (1, 0)):
                        last = M.matmul(to, left(a, k), right(z, k), start=start and n == 0, stop=stop and n == 5, skip_group_check=skip)
                        n += 1
                return last

            def bias(to, at, n):
                M.matmul(to, ones_r[:, :], bias_r[:, at:at + n], start=True, stop=False)

            pe.wait_ge(s["folds_loaded"], 64)
            for bank, left, right in ((0, wq_s, rT_s), (2, lT_s, wwT_s)):
                for m in range(KD):
                    for k in range(KD):
                        last = M.matmul(PS[:, bank + m, 0:D], left[:, k, m * P:(m + 1) * P], right[:, k, :], start=k == 0, stop=k == KD - 1)
            last.then_inc(s["fold_done"], 1)
            pe.wait_ge(s["const_done"], 1)
            pe.wait_ge(s["consts_ready"], 1)
            pe.wait_ge(s["bias_ready"], 16)
            pe.wait_ge(s["ones_stored"], 16 * NC_)
            pe.wait_ge(s["low_done"], 1)

            def tile(kind, j, bt):
                sl = j % 2
                if (kind, j) in TILE_USE:
                    n = TILE_USE[kind, j]
                    if n > 0:
                        before, i = USES[n - 1]
                        W(pe, LAST_READ[before], bt, TB, i + 1)
                if kind == "T1":
                    W(pe, "xn_ready", bt, TB, j + 1)
                    for k in range(KD):
                        last = M.transpose(PS[:, TILE, k * P:(k + 1) * P], xn[sl][:, k * P:(k + 1) * P], ident[:, :])
                    last.then_inc(s["xT_done"], 1)
                elif kind in ("T2", "T3"):
                    left = lambda a, k: xnT[sl][:, a, k, :]
                    if kind == "T2":
                        W(pe, "xlow_ready", bt, TB, j + 1)
                        bias(PS[:, TILE, :], BQKV, C)
                        three(PS[:, TILE, :], left, lambda z, k: wqkv_r[:, z, k, 0:C], False).then_inc(s["proj1_done"], 1)
                    else:
                        bias(PS[:, TILE, 0:D], BQKV + C, D)
                        three(PS[:, TILE, 0:D], left, lambda z, k: wqkv_r[:, z, k, C:3 * D], False)
                        three(PS[:, TILE, D:2 * D], left, lambda z, k: rq_r[:, z, k, :], True).then_inc(s["proj2_done"], 1)
                elif kind == "K0":
                    W(pe, "leaf_ready", bt, TB, j + 1)
                    W(pe, "ctx_ready", bt, TB, j + 1)
                    c, lf = ctx0[sl].rearrange("p h d -> p (h d)"), leaf[sl].rearrange("p n c -> p (n c)")
                    for k in range(4):
                        a = (c, lf)[k // 2]
                        last = M.transpose(PS[:, TILE, k * P:(k + 1) * P], a[:, k % 2 * P:(k % 2 + 1) * P], ident[:, :])
                    last.then_inc(s["backT_done"], 1)
                elif kind == "K1":
                    W(pe, "clow_ready", bt, TB, j + 1)
                    to = PS[:, TILE, 0:D]
                    bias(to, BOUT, D)
                    three(to, lambda a, k: clT[sl][:, a, k, :], lambda z, k: wout_r[:, z, k, :], False, stop=False)
                    three(to, lambda a, k: clT[sl][:, a, 2 + k, :], lambda z, k: lw_r[:, z, k, :], False).then_inc(s["out_done"], 1)

            def expert(kind, q, b):
                v, f = divmod(q, 2)
                e, c = divmod(v, 2)
                if kind in ("G", "U"):
                    n = 2 * q + (kind == "U")
                    if kind == "G" and q == 4 * e:
                        W(pe, ew[e % 2], b, 16 * 5, 16 * (e // 2 + 1))
                    if n >= 3:
                        W(pe, "hs_ready" if (n - 3) % 2 else "silu_done", b, NQ, (n - 3) // 2 + 1)
                    o = (n % 2) * FF + f * P
                    three(PS[:, n % 3, :], lambda a, k: ww[e % 2][:, a, k, o:o + P], lambda z, k: xbT[:, z, k, c * C:(c + 1) * C],
                          True).then_inc(s["gu_done"], 1)
                elif kind == "D":
                    m = f
                    W(pe, "hlow_ready", b, NQ, 2 * v + 2)
                    three(PS[:, ACC + 2 * m + c, :], lambda a, k: ww[e % 2][:, a, k, 2 * FF + m * P:2 * FF + (m + 1) * P],
                          lambda z, k: HR[v % 2][:, z, k, :], e == 0, stop=e == EA - 1).then_inc(s["y_done"], 1)

            def both(b, events):
                for kind, n in events:
                    if kind[0] in "THK":
                        tile(kind, n, b + 1)
                    else:
                        expert(kind, n, b)
                W(pe, "y_evac", b, 1, 1)
                for j in range(TB):
                    W(pe, "y_added", b, TB, j - 1)
                    for m in range(KD):
                        last = M.transpose(PS[:, j % 2, m * P:(m + 1) * P], YT[:, m, j // 4, (j % 4) * P:(j % 4 + 1) * P], ident[:, :])
                    last.then_inc(s["yT_done"], 1)

            def attention(b):
                for j in range(TB):
                    W(pe, "ln_ready", b, TB, j + 1)
                    W(pe, "blow2_ready", b, TB, j - 1)
                    for k in range(KD):
                        last = M.transpose(PS[:, 4 + j % 2, k * P:(k + 1) * P], xn2[j % 2][:, k * P:(k + 1) * P], ident[:, :])
                    last.then_inc(s["lnT_done"], 1)
                for u in range(8):
                    m, c = KQ_ORDER[u // 2], u % 2
                    if u == 0:
                        W(pe, "blow2_ready", b, TB, TB)
                    W(pe, "kq_evac", b, 8, u - 3)
                    three(PS[:, u % 4, :], lambda a, k: wkqv_r[:, a, k, m * P:(m + 1) * P], lambda z, k: xbT[:, z, k, c * C:(c + 1) * C],
                          True).then_inc(s["kq_done"], 1)
                for j in range(TB):
                    W(pe, "v_evac", b, TB, j - 1)
                    left = lambda a, k: xbT[:, a, k, j * P:(j + 1) * P]
                    to = PS[:, 4 + j % 2, 0:D]
                    bias(to, BV, D)
                    three(to, left, lambda z, k: wkqv_r[:, z, k, 2 * D:3 * D], False)
                    three(PS[:, 4 + j % 2, D:D + E], left, lambda z, k: rw_r[:, z, k, :], True).then_inc(s["v_done"], 1)
                W(pe, "kq_evac", b, 8, 8)

                for kind, g, u in ATTENTION:
                    Q, K = QS[g % 2], KS[g % 2]
                    if kind == "A":
                        hh, i, part = units[u]
                        w = min(C, (i + 1) * P - part * C)
                        if u == 0:
                            W(pe, stack[g % 2], b, 2 * 192, 192 * (g // 2 + 1))
                        W(pe, "a_maxed", b, NG * NU, g * NU + u - 1)
                        diag = (i + 1) * P - part * C <= C
                        last = M.matmul(PS[:, u % 2, 0:w], Q[0:ROWS, hh, i * P:(i + 1) * P], K[0:ROWS, hh, part * C:part * C + w],
                                        start=True, stop=not diag)
                        if diag:
                            last = M.matmul(PS[:, u % 2, w - P:w], identb[:, :], mask_n[:, :], start=False, stop=True)
                        last.then_inc(s["a_scored"], 1)
                    elif kind == "N":
                        W(pe, "ns_ready", b, NG, g + 1)
                        W(pe, "cn_done", b, 2 * NG, 2 * (g - 1) + 1)
                        for c in range(2):
                            if c == 1:
                                W(pe, "nr_ready", b, 2 * NG, 2 * g + 1)
                            for j in range(4):
                                last = M.transpose(PS[0:3 * G4, 2, j * P:(j + 1) * P], ns[:, 4 * c + j, :, :].rearrange("p a h -> p (a h)"), ident[:, :])
                            last.then_inc(s["nsT_done"], 1)
                    elif kind == "R":
                        W(pe, "cmb_ready", b, 1, 1)
                        W(pe, "nr_ready", b, 2 * NG, 2)
                        for c in range(2):
                            W(pe, "cmbT_ready", b, 2, c)
                            for j in range(4):
                                last = M.transpose(PS[0:E, 2, j * P:(j + 1) * P], CMB[:, 4 * c + j, :], ident[:, :])
                            last.then_inc(s["cmbT_done"], 1)
                    elif kind == "S":
                        qc, kt = steps[u]
                        q0, w = q_span(qc, kt)
                        if u == 0:
                            W(pe, neg[g % 2], b, 32, 16 * (g // 2 + 1))
                        for p in range(2):
                            W(pe, "p_ready", b, 2 * NG * NS_, 2 * (g * NS_ + u) + p - 1)
                            for hh in (2 * p, 2 * p + 1):
                                diag = q0 == kt * P
                                last = M.matmul(PS[:, 3 + hh, 0:w], K[0:ROWS_M, hh, kt * P:(kt + 1) * P], Q[0:ROWS_M, hh, q0:q0 + w],
                                                start=True, stop=not diag)
                                if diag:
                                    last = M.matmul(PS[:, 3 + hh, 0:P], identb[:, :], mask_t[:, :], start=False, stop=True)
                            last.then_inc(s["s_scored"], 1)
                    elif kind == "PV":
                        qc, kt = steps[u]
                        q0, w = q_span(qc, kt)
                        W(pe, "p_ready", b, 2 * NG * NS_, 2 * (g * NS_ + u) + 2)
                        if kt == 0:
                            W(pe, "c_evac", b, 2 * NG, 2 * g + qc)
                            if g == 0:
                                W(pe, "v_evac", b, TB, TB)
                        for hh in range(G4):
                            last = M.matmul(PS[32 * hh:32 * hh + 32, 7, q0 - qc * C:q0 - qc * C + w], vaug[:, kt, g * G4 + hh, :],
                                            PT[u % 2][:, hh, 0:w], start=kt == 0, stop=kt == 4 * qc + 3)
                        last.then_inc(s["pv_done"], 1)
                    elif kind == "CT":
                        k = 2 * g + u
                        W(pe, "c_evac", b, 2 * NG, k + 1)
                        W(pe, "cn_done", b, 2 * NG, k)
                        W(pe, "nr_ready", b, 2 * NG, 2 * min(NG, g + 1 + u))
                        W(pe, "cmbT_ready", b, 2, 2)
                        for j in range(4):
                            last = M.transpose(PS[:, 2, j * P:(j + 1) * P], CA[:, j * P:(j + 1) * P], ident[:, :])
                        last.then_inc(s["ctxT_done"], 1)
                W(pe, "cn_done", b, 2 * NG, 2 * NG)
                for j in range(TB + 1):
                    if j < TB:
                        W(pe, "wolow_ready", b, TB, j - 1)
                        for k in range(KD):
                            last = M.transpose(PS[:, 2 + j % 2, k * P:(k + 1) * P], ctxN[:, j, k * P:(k + 1) * P], ident[:, :])
                        last.then_inc(s["woT_done"], 1)
                    if j > 0:
                        i = j - 1
                        W(pe, "wolow_ready", b, TB, i + 1)
                        W(pe, "wo_added", b, TB, i - 1)
                        to = PS[:, 4 + i % 2, 0:D]
                        bias(to, BO, D)
                        three(to, lambda a, k: cT[i % 2][:, a, k, :], lambda z, k: wo_r[:, z, k, :], False).then_inc(s["wo_done"], 1)
                W(pe, "wo_added", b, TB, TB)

            for kind, j in TILES:
                tile(kind, j, 0)
            with pe.Fori(0, B - 1) as b:
                attention(b)
                both(b, BOTH)
            attention(B - 1)
            both(B - 1, EXPERTS)



def kernel(**inputs):
    import numpy as np
    import concourse.bacc as bacc
    from concourse.bass_utils import run_bass_kernel_spmd

    a = {k: np.asarray(v) for k, v in inputs.items()}
    blocks = lambda w: np.stack([w[:, i * FF:(i + 1) * FF] for i in range(ES)])
    laid = {
        "x": a["L0_attn_x"].reshape(N, D),
        "w_qkv": a["L0_attn_W_qkv"], "b_qkv": a["L0_attn_b_qkv"],
        "w_out": a["L0_attn_W_out"], "b_out0": a["L0_attn_b_out"],
        "wq": a["L0_ffn_Wq"], "routersT": np.pad(a["L0_ffn_routers"].T, ((0, 0), (0, 1))), "leafT": a["L0_ffn_leaf_values"].T,
        "woutT": a["L0_ffn_Wout_w"].T, "wout_b": a["L0_ffn_Wout_b"],
        "w_kqv": a["L1_attn_W_kqv"], "b_kqv": a["L1_attn_b_kqv"],
        "b_kq": a["L1_attn_b_kqv"][:2 * D].reshape(4, P).T,
        "w_o": a["L1_attn_W_o"], "b_o": a["L1_attn_b_o"], "router_w": a["L1_ffn_router_w"],
        "w_gate": np.concatenate([a["L1_ffn_gate_w"], blocks(a["L1_ffn_shared_gate_w"])]),
        "w_up": np.concatenate([a["L1_ffn_up_w"], blocks(a["L1_ffn_shared_up_w"])]),
        "w_down": np.concatenate([a["L1_ffn_down_w"], a["L1_ffn_shared_down_w"].reshape(ES, FF, D)]),
    }
    nc = bacc.Bacc("TRN2", target_bir_lowering=False, num_devices=1)
    laid = {k: np.ascontiguousarray(v) for k, v in laid.items()}
    aps = [nc.dram_tensor(f"in_{k}", v.shape, mybir.dt.from_np(v.dtype), kind="ExternalInput").ap() for k, v in laid.items()]
    out = nc.dram_tensor("out_0", (N, D), F32, kind="ExternalOutput").ap()
    build(nc, *aps, out)
    r = run_bass_kernel_spmd(nc, [{f"in_{k}": v for k, v in laid.items()}], core_ids=[0])
    return r.results[0]["out_0"].reshape(B, T, D)
```

```python
from contextlib import ExitStack

import concourse.bass as bass
from concourse import mybir

F32 = mybir.dt.float32
BF16 = mybir.dt.bfloat16
F32R = mybir.dt.float32r
ACT = mybir.ActivationFunctionType
ALU = mybir.AluOpType
AX = mybir.AxisListType

P = 128
B, T, D = 4, 1024, 256
N = B * T
NT = N // P
TB = T // P
KD = D // P
H, DK = 16, 16
NODE = 255
DEPTH = 8
E, ES = 8, 2
EA = E + ES
FF = 256
C = 512
NC_ = T // C
EPS = 1e-5
SCALE = 1.0 / DK ** 0.5
NEG = -1.0e30
LOWEST = -3.0e38
HP = 8
G4 = 4
NG = H // G4
PAIRS = [(0, 0), (0, 1), (1, 0), (1, 1), (0, 2), (2, 0)]
ROWS = len(PAIRS) * DK
ROWS_M = ROWS + 3


class Steps:

    def __init__(self, eng, sem):
        self.eng, self.sem, self.at, self.n, self.outer = eng, sem, 0, 0, []

    def did(self, instruction):
        instruction.then_inc(self.sem, 1)
        self.n += 1
        self.eng.wait_ge(self.sem, self.at + self.n)

    def enter(self, i, per):
        self.outer.append((self.at, self.n))
        self.at, self.n = self.at + self.n + i * per, 0

    def leave(self, count, per):
        assert self.n == per, (self.n, per)
        self.at, self.n = self.outer.pop()
        self.n += count * per


def spread(main, other):
    merged, k = [], 0
    for i, item in enumerate(main):
        merged.append(item)
        upto = len(other) * (i + 1) // len(main)
        merged += other[k:upto]
        k = upto
    return merged


steps = [(qc, kt) for qc in range(NC_) for kt in range(4 * (qc + 1))]
units = [(hh, i, part) for hh in range(G4) for i in range(TB) for part in range(1 + (i >= 4))]
NS_, NU = len(steps), len(units)
AT = NU // 8
KQ_ORDER = [0, 2, 1, 3]
NV = NC_ * EA
NQ = 2 * NV


def outputs(first, end):
    return [(e, 0, j - lag) for j in range(first, end + 1) for e, lag in (("O1", 0), ("O3", 1), ("O2", 0), ("O4", 1))
            if first <= j - lag < end]


def attention_order():
    order = [("A", 0, u) for u in range(NU)] + [("N", 0, 0), ("NT", 0, 0), ("R", 0, 0)]
    early = outputs(0, TB // 2)
    pending = None
    for g in range(NG):
        order += [("S0", g, 0), ("S1", g, 0)]
        for t in range(NS_):
            found = []
            if g + 1 < NG:
                found = [("A", g + 1, u) for u in range(AT * t, min(NU, AT * t + AT))]
                if AT * t < NU <= AT * t + AT:
                    found.append(("N", g + 1, 0))
            more = t + 1 < NS_
            order += found[0:2] + [("S0", g, t + 1)] * more + found[2:3] + [("S1", g, t + 1)] * more
            order += found[3:4] + [("PV", g, t)] + found[4:]
            if pending:
                order.append(pending)
                pending = None
            if AT * (t - 1) < NU <= AT * t and g + 1 < NG:
                order.append(("NT", g + 1, 0))
            if g + 1 == NG and t >= 5:
                order += early[:3]
                del early[:3]
            if t + 1 == NS_ or steps[t + 1][0] != steps[t][0]:
                order.append(("CE", g, steps[t][0]))
                pending = ("CT", g, steps[t][0])
            if g == 0 and t == 0:
                order.append(("STATS", 0, 0))
            if g == 0 and t == 2:
                order.append(("RT", 0, 0))
    return order + early + [pending] + outputs(TB // 2, TB)


def tile_order():
    order = [(e, 0) for e in ("T0", "T1", "T1L", "T2", "T3")]
    for j in range(TB):
        back, more = j > 0, j + 1 < TB
        for e in ("H0", "H1", "K0", "H2", "T0", "K0L", "H3", "K1", "H4", "K1A", "T1", "H5", "T1L", "H6",
                  "T2", "H7", "H8", "T3", "H9", "H10"):
            if e[0] == "H":
                order.append((e, j))
            elif e[0] == "K" and back:
                order.append((e, j - 1))
            elif e[0] == "T" and more:
                order.append((e, j + 1))
    return order + [(e, TB - 1) for e in ("K0", "K0L", "K1", "K1A")]


def expert_order():
    order = []
    for q in range(NQ + 2):
        for e, lag in (("G", 0), ("X", 1), ("U", 0), ("D", 2), ("M", 0)):
            if 0 <= q - lag < NQ:
                order.append((e, q - lag))
    return order


ATTENTION, TILES, EXPERTS = attention_order(), tile_order(), expert_order()
BOTH = spread(EXPERTS, TILES)
USES = [e for e in TILES if e[0] in ("T1", "T2", "T3", "K0", "K1")]
TILE_USE = {e: n for n, e in enumerate(USES)}
LAST_READ = {"T1": "xlow_ready", "T2": "half_ready", "T3": "tanh_done", "K0": "clow_ready", "K1": "x2_done"}
OWN = [(HP, HP + (H - HP + 1) // 2), (HP + (H - HP + 1) // 2, H)]
SHARE = [(0, 3), (3, 6), (6, HP)]


def a_banks(g):
    return (0, 1, 3, 4, 5, 6) if g == 0 else (0, 1)


def output_banks(u):
    if u <= TB // 2:
        return 0, 1, u
    return (0, 3)[u % 2], (1, 4)[u % 2], u - 1


def q_span(qc, kt):
    first = max(qc * C, kt * P)
    return first, (qc + 1) * C - first


def build(nc, x, w_qkv, b_qkv, w_out, b_out0, wq, routersT, leafT, woutT, wout_b, w_kqv, b_kqv, b_kq, w_o,
          b_o, router_w, w_gate, w_up, w_down, out):
    ctx = ExitStack()
    with ctx:
        def sb(name, shape, dt=F32):
            return ctx.enter_context(nc.sbuf_tensor(name, shape, dt))

        xs = sb("xs", [P, NT, D])
        wqkv_r = sb("wqkv_r", [P, 2, KD, 3 * D], F32R)
        rq_r = sb("rq_r", [P, 2, KD, D], F32R)
        wout_r = sb("wout_r", [P, 2, KD, D], F32R)
        lw_r = sb("lw_r", [P, 2, KD, D], F32R)
        wkqv_r = sb("wkqv_r", [P, 2, KD, 3 * D], F32R)
        wo_r = sb("wo_r", [P, 2, KD, D], F32R)
        rw_r = sb("rw_r", [P, 2, KD, E], F32R)
        rw_s = sb("rw_s", [P, KD, E])
        bias_r = sb("bias_r", [2, 6 * D], F32R)
        BQKV, BOUT, BV, BO = 0, 3 * D, 4 * D, 5 * D
        ones_r = sb("ones_r", [2, P], F32R)
        bkq = sb("bkq", [P, 4])
        ident = sb("ident", [P, P])
        identb = sb("identb", [P, P], BF16)
        mask_n = sb("mask_n", [P, P], BF16)
        mask_t = sb("mask_t", [P, P], BF16)
        one = sb("one", [P, 1])
        pause = sb("pause", [P, 1])
        idle = sb("idle", [P, 3])
        half = sb("half", [P, TB])
        st = sb("st", [P, 2 * TB, 6])
        mv = sb("mv", [P, 2 * TB, 2])
        var = sb("var", [P, 2 * TB])
        rstd = sb("rstd", [P, 2 * TB])
        xbT = sb("xbT", [P, 2, KD, T], F32R)
        nmp = sb("nmp", [P, G4, TB, 2])
        nm = sb("nm", [P, TB, G4])
        nmr = sb("nmr", [P, TB, G4])
        nmb = sb("nmb", [P, TB, G4], BF16)
        ns = sb("ns", [P, TB, 3, G4])
        rc = sb("rc", [P, G4, G4])
        LG = sb("LG", [P, TB, E])
        LP = sb("LP", [P, TB, E])
        CMB = sb("CMB", [P, TB, E])
        lmax = sb("lmax", [P, TB])
        lsum = sb("lsum", [P, TB])
        top8 = sb("top8", [P, TB, 8])
        rep8 = sb("rep8", [P, TB, 8])
        xn2 = [sb(f"xn2_{i}", [P, D]) for i in range(2)]

        AREA = 26944
        base = nc.sbuf_base
        arena = sb("arena", [P, AREA])
        free, pieces = [0], []

        def take(shape, dt=F32, rows=P):
            words = 1
            for n in shape:
                words *= n
            if dt == BF16:
                words //= 2
            pieces.append(nc.alloc_sbuf_tensor_at(f"piece{len(pieces)}", [rows, *shape], dt, offset=base + 4 * free[0]))
            free[0] += (words + 7) // 8 * 8
            assert free[0] <= AREA, free[0]
            return pieces[-1][(slice(None),) * (1 + len(shape))]

        parts = take([4, 3, T], BF16)
        QS = [take([G4, T], BF16) for _ in range(2)]
        KS = [take([G4, T], BF16) for _ in range(2)]
        rest_at, free[0] = free[0], 0
        QS.append(take([G4, T], BF16))
        KS.append(take([G4, T], BF16))
        assert free[0] <= 4 * 3 * T // 2
        free[0] = 4 * 3 * T // 2 + G4 * T // 2
        cT = [take([2, KD, P], F32R) for _ in range(2)]
        free[0] = rest_at
        pt_at = free[0]
        PT = [take([G4, C]) for _ in range(2)]
        vaug = take([TB, H, 32])
        ctxN = take([TB, D])
        CA = take([C])
        NR = take([T], BF16, rows=3 * G4)
        cT8 = take([T], rows=E)
        free[0] = pt_at
        XF = [take([C]) for _ in range(2)]
        RR = take([C])
        free[0] = 0
        ww = [take([2, KD, 3 * FF], F32R) for _ in range(2)]
        assert free[0] <= 3 * 4 * T // 2
        cb = [take([T]) for _ in range(2)]
        SG = [take([C]) for _ in range(2)]
        HS = [take([C]) for _ in range(2)]
        HF = [take([C]) for _ in range(2)]
        h_at = free[0]
        HR = [take([2, C], F32R) for _ in range(4)]
        tiles_at = free[0]
        free[0] = h_at
        YT = take([KD, NC_, C])
        free[0] = tiles_at
        prod = take([H, H, DK])
        qkv = [take([H, 3, DK]) for _ in range(2)]
        gates = [take([D]) for _ in range(2)]
        xn = [take([D]) for _ in range(2)]
        xnT = [take([2, KD, P], F32R) for _ in range(2)]
        att = take([H, H])
        prob = take([H, H])
        mx = take([H])
        sums = take([H])
        ctx0 = [take([H, DK]) for _ in range(2)]
        tree = [take([2 ** l]) for l in range(1, DEPTH)]
        leaf = [take([D // 2, 2]) for _ in range(2)]
        clT = [take([2, 4, P], F32R) for _ in range(2)]
        free[0] = 0
        wq_s, rT_s, lT_s, wwT_s = (take([KD, D]) for _ in range(4))
        wqkv_s, wkqv_s = (take([KD, 3 * D]) for _ in range(2))
        wout_s, wo_s = (take([KD, D]) for _ in range(2))
        eraw = [take([KD, 3 * FF]) for _ in range(2)]
        ehl = [take([2, KD, 3 * FF], F32R) for _ in range(2)]
        assert free[0] <= tiles_at
        free[0] = tiles_at
        braw = take([7 * D], rows=1)
        blow = take([6 * D], F32R, rows=1)
        plain_ones = take([C], rows=ES)

        PS = ctx.enter_context(nc.psum_tensor("PS", [P, 8, C], F32))
        ACC, TILE = 3, 7

        scr_parts = nc.dram_tensor("scr_parts", (4, P, 3, T), BF16).ap()
        scr_ones = nc.dram_tensor("scr_ones", (3 * G4, T), BF16).ap()
        scr_cmb = nc.dram_tensor("scr_cmb", (EA, T), F32).ap()
        scr_w = nc.dram_tensor("scr_w", (EA, P, 2, KD, 3 * FF), F32).ap()

        s = {name: ctx.enter_context(nc.semaphore(name)) for name in (
            "folds_loaded x_loaded others_loaded wqkv_loaded w_loaded const_done fold_done high_done low_done rest_done brow_loaded "
            "bsum_ready blow_ready bias_ready ones_stored consts_ready eraw0 eraw1 ehigh_done elow0 elow1 e_stored0 e_stored1 "
            "d_step p_step "
            "var_ready rstd_ready xn_ready xT_done xhigh_ready xlow_ready half_ready proj1_done "
            "proj2_done qkv_ready tanh_done gate_ready mulp_done part_reduced shifted probs_ready "
            "leaf_ready ctx_ready backT_done chigh_ready clow_ready out_done x2_done "
            "aug_ready ln_ready lnT_done bhigh_ready blow2_ready kq_done kq_evac parts_ready "
            "parts_stored v_done v_evac lshifted lprobs_ready cmb_ready cmbT_done cmbT_ready "
            "cmb_stored stack0 stack1 stack2 neg0 neg1 neg2 a_scored a_maxed ns_ready nsT_done nr_ready "
            "s_scored p_ready pv_done c_evac ctxT_done cn_done woT_done wohigh_ready wolow_ready "
            "wo_done wo_added "
            "ew0 ew1 ec0 ec1 gu_done silu_done hs_ready hf_ready hhigh_ready hlow_ready y_done "
            "y_evac yT_done y_added stored").split()}
        stack, neg = [s["stack0"], s["stack1"], s["stack2"]], [s["neg0"], s["neg1"], s["neg2"]]
        eraw_loaded = [s["eraw0"], s["eraw1"]]
        elow_done = [s["elow0"], s["elow1"]]
        e_stored = [s["e_stored0"], s["e_stored1"]]
        ew, ec = [s["ew0"], s["ew1"]], [s["ec0"], s["ec1"]]

        def W(eng, name, b, per, c):
            if c > 0:
                eng.wait_ge(s[name] if isinstance(name, str) else name, b * per + c)

        block = ctx.enter_context(nc.Block())

        @block.sync
        def _(sp):
            xv = x.rearrange("(n p) d -> p n d", p=P)
            wv = lambda w: w.rearrange("(k p) n -> p k n", p=P)
            row = lambda a: a.rearrange("(o n) -> o n", o=1)
            sp.dma_start(xs[:, 0:TB, :], xv[:, 0:TB, :]).then_inc(s["x_loaded"], 16)
            for dst, src in ((wq_s, wq), (rT_s, routersT), (lT_s, leafT), (wwT_s, woutT)):
                sp.dma_start(dst, wv(src)).then_inc(s["folds_loaded"], 16)
            sp.wait_ge(s["consts_ready"], 1)
            sp.dma_start(scr_ones, NR).then_inc(s["ones_stored"], 16)
            for c in range(NC_):
                sp.dma_start(scr_cmb[E:EA, c * C:(c + 1) * C], plain_ones).then_inc(s["ones_stored"], 16)
            for o, src in ((0, b_qkv), (3 * D, b_out0), (6 * D, wout_b), (5 * D, b_o)):
                sp.dma_start(braw[:, o:o + src.shape[0]], row(src)).then_inc(s["brow_loaded"], 16)
            sp.dma_start(braw[:, 4 * D:5 * D], row(b_kqv)[:, 2 * D:3 * D]).then_inc(s["brow_loaded"], 16)
            sp.dma_start(wqkv_s, wv(w_qkv)).then_inc(s["wqkv_loaded"], 16)
            for dst, src in ((wout_s, w_out), (wkqv_s, w_kqv), (wo_s, w_o), (rw_s[:, :, :], router_w)):
                sp.dma_start(dst, wv(src)).then_inc(s["w_loaded"], 16)
            sp.dma_start(bkq[:, :], b_kq).then_inc(s["w_loaded"], 16)
            for e in range(EA + 1):
                if e < EA:
                    if e >= 2:
                        sp.wait_ge(elow_done[e % 2], e // 2)
                    for o, w in enumerate((w_gate, w_up, w_down)):
                        sp.dma_start(eraw[e % 2][:, :, o * FF:(o + 1) * FF], wv(w[e])).then_inc(eraw_loaded[e % 2], 16)
                if e == 1:
                    for i in range(1, B):
                        sp.dma_start(xs[:, i * TB:(i + 1) * TB, :], xv[:, i * TB:(i + 1) * TB, :]).then_inc(s["others_loaded"], 16)
                if e >= 1:
                    sp.wait_ge(elow_done[(e - 1) % 2], (e - 1) // 2 + 1)
                    sp.dma_start(scr_w[e - 1], ehl[(e - 1) % 2].bitcast(F32)).then_inc(e_stored[(e - 1) % 2], 16)

            def attention(b):
                def store_parts(n):
                    W(sp, "parts_ready", b, 8, 4 * n + 4)
                    for blk in KQ_ORDER[2 * n:2 * n + 2]:
                        sp.dma_start(scr_parts[blk], parts[:, blk, :, :]).then_inc(s["parts_stored"], 16)

                def load_stack(g):
                    if g % 2 == 0:
                        W(sp, "parts_stored", b, 64, 32 * (g // 2) + 32)
                    W(sp, "pv_done", b, NG * NS_, NS_ * (g - 2))
                    p0 = (g % 2) * G4 * DK
                    for dst, base, side in ((KS, 0, 1), (QS, 2, 0)):
                        for r, pair in enumerate(PAIRS):
                            src = scr_parts[base + g // 2, p0:p0 + G4 * DK, pair[side], :]
                            sp.dma_start(dst[g % 3][r * DK:(r + 1) * DK, :, :],
                                         src.rearrange("(h d) t -> d h t", d=DK)).then_inc(stack[g % 3], 16)
                    if g < 3:
                        sp.dma_start(KS[g][ROWS:ROWS_M, :, :], scr_ones.rearrange("(p h) t -> p h t", h=G4)).then_inc(stack[g], 16)

                def load_neg(g):
                    W(sp, "nr_ready", b, 2 * NG, 2 * g + 2)
                    for p in range(3):
                        sp.dma_start(QS[g % 3][ROWS + p:ROWS + p + 1, :, :], NR[p * G4:(p + 1) * G4, :]).then_inc(neg[g % 3], 16)

                store_parts(0)
                load_stack(0)
                load_stack(1)
                store_parts(1)
                load_neg(0)
                W(sp, "cmbT_ready", b, 2, 2)
                sp.dma_start(scr_cmb[0:E, :], cT8).then_inc(s["cmb_stored"], 16)
                load_stack(2)
                load_neg(1)
                load_stack(3)
                load_neg(2)
                load_neg(3)

            def load_cb(e, slot):
                src = scr_cmb[bass.ds(e, 1), :].partition_broadcast(P).rearrange("p o t -> p (o t)")
                sp.dma_start(cb[slot], src).then_inc(ec[slot], 16)

            def experts(b):
                W(sp, "pv_done", b, NG * NS_, NG * NS_)
                W(sp, "cmb_stored", b, 16, 16)
                for e in range(2):
                    load_cb(e, e)
                for e in range(2, EA):
                    W(sp, "hf_ready", b, NQ, 4 * (e - 1))
                    load_cb(e, e % 2)
                W(sp, "y_added", b, TB, TB)
                ov = out.rearrange("(b n p) d -> b p n d", p=P, b=B)
                sp.dma_start(ov[bass.ds(b, 1), :, :, :].rearrange("o p n d -> p (o n) d"),
                             xs[:, bass.ds(b * TB, TB), :]).then_inc(s["stored"], 16)

            for slot in range(2):
                sp.wait_ge(e_stored[slot], 16 * (EA // 2))
            with sp.Fori(0, B - 1) as b:
                attention(b)
                experts(b)
            attention(B - 1)
            experts(B - 1)
            sp.wait_ge(s["stored"], B * 16)

        @block.gpsimd
        def _(pool):
            G = nc.gpsimd
            step = Steps(pool, s["p_step"])
            step.did(G.memset(ident[:, :], 0.0))
            step.did(G.affine_select(out=ident[:, :], in_=ident[:, :], compare_op=ALU.not_equal, fill=1.0,
                                     base=0, pattern=[[-1, P]], channel_multiplier=1))
            G.memset(NR, 1.0)
            step.did(G.memset(plain_ones, 1.0))
            G.tensor_scalar(ones_r[:, :], plain_ones[:, 0:P], 1.0, None, ALU.mult).then_inc(s["consts_ready"], 1)
            G.memset(one[:, :], 1.0)
            step.did(G.memset(half[:, :], -0.5))
            step.did(G.memset(mask_n[:, :], 0.0))
            step.did(G.memset(mask_t[:, :], 0.0))
            step.did(G.affine_select(out=mask_n[:, :], in_=mask_n[:, :], compare_op=ALU.is_ge, fill=NEG,
                                     base=0, pattern=[[-1, P]], channel_multiplier=1))
            step.did(G.affine_select(out=mask_t[:, :], in_=mask_t[:, :], compare_op=ALU.is_ge, fill=NEG,
                                     base=0, pattern=[[1, P]], channel_multiplier=-1))
            G.tensor_scalar(identb[:, :], ident[:, :], 1.0, None, ALU.mult).then_inc(s["const_done"], 1)

            def power(n, sl):
                pool.wait_ge(s["var_ready"], n)
                lo = sl * TB
                G.tensor_tensor(rstd[:, lo:lo + TB], var[:, lo:lo + TB], half[:, :], ALU.pow).then_inc(s["rstd_ready"], 1)

            def tile(kind, j, bt):
                if kind[0] != "H":
                    return
                h, sl, g = int(kind[1:]), j % 2, gates[j % 2]
                q, k, v = (qkv[sl][:, :, i, :] for i in range(3))
                if h < len(SHARE):
                    a, z = SHARE[h]
                    if h == 0:
                        W(pool, "qkv_ready", bt, TB, j + 1)
                        W(pool, "part_reduced", bt, 2 * TB, 2 * j)
                    i = G.tensor_tensor(prod[:, a:z, :, :], q[:, a:z, :].unsqueeze(2).to_broadcast([P, z - a, H, DK]),
                                        k.unsqueeze(1).to_broadcast([P, z - a, H, DK]), ALU.mult)
                    if h == len(SHARE) - 1:
                        i.then_inc(s["mulp_done"], 1)
                levels = {3: range(0, 5), 4: range(5, 6), 5: range(6, 7), 9: range(7, 8)}.get(h, ())
                for l in levels:
                    m = 2 ** l
                    if l == 0:
                        W(pool, "gate_ready", bt, TB, j + 1)
                        G.tensor_tensor(tree[0][:, 0:1], one[:, :], g[:, 0:1], ALU.subtract)
                        step.did(G.tensor_tensor(tree[0][:, 1:2], one[:, :], g[:, 0:1], ALU.mult))
                        continue
                    if l == DEPTH - 1:
                        W(pool, "backT_done", bt, TB, j - 1)
                    to = leaf[sl] if l == DEPTH - 1 else tree[l].rearrange("p (n c) -> p n c", c=2)
                    step.did(G.tensor_tensor(to[:, :, 1], tree[l - 1], g[:, m - 1:2 * m - 1], ALU.mult))
                    i = G.tensor_tensor(to[:, :, 0], tree[l - 1], to[:, :, 1], ALU.subtract)
                    if l < DEPTH - 1:
                        step.did(i)
                    else:
                        i.then_inc(s["leaf_ready"], 1)
                if 6 <= h < 6 + len(SHARE):
                    a, z = SHARE[h - 6]
                    if h == 6:
                        W(pool, "probs_ready", bt, TB, j + 1)
                        W(pool, "part_reduced", bt, 2 * TB, 2 * j + 1)
                    i = G.tensor_tensor(prod[:, a:z, :, :], prob[:, a:z, :].unsqueeze(2).to_broadcast([P, z - a, DK, H]),
                                        v.rearrange("p g d -> p d g").unsqueeze(1).to_broadcast([P, z - a, DK, H]), ALU.mult)
                    if h - 6 == len(SHARE) - 1:
                        i.then_inc(s["mulp_done"], 1)

            def expert(kind, q, b):
                if kind != "M":
                    return
                v = q // 2
                e, c = divmod(v, 2)
                if q % 4 == 2 and 2 <= e + 1 < EA:
                    W(pool, "y_done", b, NQ, 4 * e)
                    rest(2)
                    load_weights(e + 1)
                if v % 2 == 0 and q % 2 == 0:
                    W(pool, ec[e % 2], b, 16 * 5, 16 * (e // 2 + 1))
                W(pool, "hs_ready", b, NQ, q + 1)
                W(pool, "hlow_ready", b, NQ, q - 1)
                G.tensor_tensor(HF[q % 2], HS[q % 2], cb[e % 2][:, c * C:(c + 1) * C], ALU.mult).then_inc(s["hf_ready"], 1)

            def rest(i):
                G.tensor_tensor(idle[:, i:i + 1], one[:, :], one[:, :], ALU.mult)

            def load_weights(e):
                G.dma_start(ww[e % 2], scr_w[e]).then_inc(ew[e % 2], 16)

            def both(b, events):
                for kind, n in events:
                    if kind[0] in "THK":
                        tile(kind, n, b + 1)
                    else:
                        expert(kind, n, b)

            def start(b):
                W(pool, "ln_ready", b, TB, 1)
                rest(0)
                G.memset(vaug[:, :, :, DK:32], 1.0).then_inc(s["aug_ready"], 1)
                W(pool, "pv_done", b, NG * NS_, 3 * NS_)
                rest(1)
                for e in range(2):
                    load_weights(e)

            pool.wait_ge(s["blow_ready"], 1)
            G.dma_start(bias_r[1:2, :], blow.bitcast(F32)).then_inc(s["bias_ready"], 16)
            power(1, 0)
            for kind, j in TILES:
                tile(kind, j, 0)
                if kind == "H9" and j < EA // 2:
                    pool.wait_ge(s["ehigh_done"], 2 * j + 2)
                    G.tensor_tensor(ehl[1][:, 1, :, :], eraw[1], ehl[1][:, 0, :, :].bitcast(F32), ALU.subtract).then_inc(elow_done[1], 1)
            per = TB * (1 + 2 * (DEPTH - 2) + 1)
            for slot in range(2):
                pool.wait_ge(e_stored[slot], 16 * (EA // 2))
            with pool.Fori(0, B - 1) as b:
                step.enter(b, per)
                power(b * 2 + 2, 1)
                start(b)
                power(b * 2 + 3, 0)
                both(b, BOTH)
                step.leave(B - 1, per)
            power(2 * B, 1)
            start(B - 1)
            both(B - 1, EXPERTS)

        @block.vector
        def _(dve):
            V = nc.vector
            step = Steps(dve, s["d_step"])

            def low(to, whole, high):
                return V.tensor_tensor(to, whole, high.bitcast(F32), ALU.subtract)

            def norm_stats(tile0, sl, first=0):
                lo = sl * TB
                V.memset(pause[:, :], 0.0)
                for j in range(first, TB):
                    i = V.bn_stats(st[:, lo + j, :], xs[:, tile0 + j, :])
                step.did(i)
                V.memset(pause[:, :], 0.0)
                for j in range(TB):
                    i = V.bn_aggr(mv[:, lo + j, :], st[:, lo + j, :])
                step.did(i)
                V.tensor_scalar(var[:, lo:lo + TB], mv[:, lo:lo + TB, 1], EPS, None, ALU.add).then_inc(s["var_ready"], 1)

            V.memset(nmp[:, :, :, :], LOWEST)
            V.memset(rep8[:, :, :], -1.0)
            dve.wait_ge(s["x_loaded"], 16)
            norm_stats(0, 0)
            dve.wait_ge(s["brow_loaded"], 5 * 16)
            V.tensor_tensor(braw[:, 3 * D:4 * D], braw[:, 3 * D:4 * D], braw[:, 6 * D:7 * D], ALU.add).then_inc(s["bsum_ready"], 1)
            dve.wait_ge(s["high_done"], 1)
            low(blow, braw[:, 0:6 * D], bias_r[0:1, :]).then_inc(s["blow_ready"], 1)
            dve.wait_ge(s["high_done"], 2)
            low(wqkv_r[:, 1, :, :], wqkv_s, wqkv_r[:, 0, :, :])
            dve.wait_ge(s["high_done"], 3)
            low(rq_r[:, 1, :, :], PS[:, 0:2, 0:D], rq_r[:, 0, :, :])
            low(lw_r[:, 1, :, :], PS[:, 2:4, 0:D], lw_r[:, 0, :, :]).then_inc(s["low_done"], 1)

            def tile(kind, j, bt):
                sl = j % 2
                q, k, v = (qkv[sl][:, :, i, :] for i in range(3))

                def scores(a, z):
                    return V.tensor_tensor(prod[:, a:z, :, :], q[:, a:z, :].unsqueeze(2).to_broadcast([P, z - a, H, DK]),
                                           k.unsqueeze(1).to_broadcast([P, z - a, H, DK]), ALU.mult)

                def values(a, z):
                    return V.tensor_tensor(prod[:, a:z, :, :], prob[:, a:z, :].unsqueeze(2).to_broadcast([P, z - a, DK, H]),
                                           v.rearrange("p g d -> p d g").unsqueeze(1).to_broadcast([P, z - a, DK, H]), ALU.mult)

                def summed(a, z):
                    return V.tensor_reduce(att[:, a:z, :], prod[:, a:z, :, :], AX.X, ALU.add)

                if kind == "T0":
                    W(dve, "xT_done", bt, TB, j - 1)
                    V.tensor_scalar(xn[sl], xs[:, bt * TB + j, :], mv[:, j, 0:1], rstd[:, j:j + 1],
                                    ALU.subtract, ALU.mult).then_inc(s["xn_ready"], 1)
                elif kind == "T1L":
                    W(dve, "xhigh_ready", bt, TB, j + 1)
                    i = low(xnT[sl][:, 1, :, :], PS[:, TILE, 0:D].rearrange("p (k t) -> p k t", k=KD), xnT[sl][:, 0, :, :])
                    i.then_inc(s["xlow_ready"], 1)
                elif kind == "H0":
                    W(dve, "qkv_ready", bt, TB, j + 1)
                    step.did(scores(*OWN[0]))
                elif kind == "H1":
                    step.did(scores(*OWN[1]))
                elif kind == "H2":
                    summed(*OWN[0])
                elif kind == "H3":
                    summed(*OWN[1])
                elif kind in ("H4", "H10"):
                    n = 2 * j + 1 + (kind == "H10")
                    W(dve, "mulp_done", bt, 2 * TB, n)
                    summed(0, HP).then_inc(s["part_reduced"], 1)
                    W(dve, "part_reduced", bt, 2 * TB, n)
                    if kind == "H10":
                        W(dve, "backT_done", bt, TB, j - 1)
                        V.tensor_tensor(ctx0[sl], att, mx.unsqueeze(2).to_broadcast([P, H, DK]), ALU.mult).then_inc(s["ctx_ready"], 1)
                elif kind == "H5":
                    step.did(V.tensor_reduce(mx, att, AX.X, ALU.max))
                    V.tensor_tensor(att, att, mx.unsqueeze(2).to_broadcast([P, H, H]), ALU.subtract).then_inc(s["shifted"], 1)
                elif kind == "H6":
                    W(dve, "probs_ready", bt, TB, j + 1)
                    step.did(V.tensor_reduce(sums, prob, AX.X, ALU.add))
                    V.reciprocal(mx, sums)
                    if j > 0:
                        V.bn_stats(st[:, TB + j - 1, :], xs[:, bt * TB + (j - 1), :])
                    step.did(values(*OWN[0]))
                elif kind == "H7":
                    step.did(values(*OWN[1]))
                elif kind == "H8":
                    summed(*OWN[0])
                elif kind == "H9":
                    summed(*OWN[1])
                elif kind == "K0L":
                    W(dve, "chigh_ready", bt, TB, j + 1)
                    i = low(clT[sl][:, 1, :, :], PS[:, TILE, :].rearrange("p (k t) -> p k t", k=4), clT[sl][:, 0, :, :])
                    i.then_inc(s["clow_ready"], 1)
                elif kind == "K1A":
                    W(dve, "out_done", bt, TB, j + 1)
                    V.tensor_tensor(xs[:, bt * TB + j, :], PS[:, TILE, 0:D], xs[:, bt * TB + j, :], ALU.add).then_inc(s["x2_done"], 1)

            def expert(kind, q, b):
                if kind == "M":
                    W(dve, "silu_done", b, NQ, q + 1)
                    W(dve, "gu_done", b, 2 * NQ, 2 * q + 2)
                    W(dve, "hf_ready", b, NQ, q - 1)
                    V.tensor_tensor(HS[q % 2], SG[q % 2], PS[:, (2 * q + 1) % 3, :], ALU.mult).then_inc(s["hs_ready"], 1)
                elif kind == "X":
                    W(dve, "hhigh_ready", b, NQ, q + 1)
                    low(HR[q % 4][:, 1, :], HF[q % 2], HR[q % 4][:, 0, :]).then_inc(s["hlow_ready"], 1)

            def both(b, events):
                for kind, n in events:
                    if kind[0] in "THK":
                        tile(kind, n, b + 1)
                    else:
                        expert(kind, n, b)
                for j in range(TB):
                    W(dve, "yT_done", b, TB, j + 1)
                    V.tensor_tensor(xs[:, b * TB + j, :], PS[:, j % 2, 0:D], xs[:, b * TB + j, :], ALU.add).then_inc(s["y_added"], 1)

            def attention(b, more):
                dve.wait_ge(s["x2_done"], b * TB + TB)
                norm_stats(b * TB, 1, TB - 1)
                dve.wait_ge(s["rstd_ready"], b * 2 + 2)
                for j in range(TB):
                    W(dve, "lnT_done", b, TB, j - 1)
                    V.tensor_scalar(xn2[j % 2][:, :], xs[:, b * TB + j, :], mv[:, TB + j, 0:1], rstd[:, TB + j:TB + j + 1],
                                    ALU.subtract, ALU.mult).then_inc(s["ln_ready"], 1)
                    if j >= 1:
                        low_xb(b, j - 1)
                low_xb(b, TB - 1)
                for u in range(8):
                    blk, c = KQ_ORDER[u // 2], u % 2
                    to = [parts[:, blk, p, c * C:(c + 1) * C] for p in range(3)]
                    W(dve, "kq_evac", b, 8, u + 1)
                    step.did(V.tensor_tensor(RR, XF[u % 2], to[0], ALU.subtract))
                    step.did(V.tensor_copy(to[1], RR))
                    V.tensor_tensor(to[2], RR, to[1], ALU.subtract).then_inc(s["parts_ready"], 1)
                    if u < 7:
                        W(dve, "parts_ready", b, 8, u + 1)

                for kind, g, u in ATTENTION:
                    if kind == "A":
                        hh, i, part = units[u]
                        w = min(C, (i + 1) * P - part * C)
                        W(dve, "a_scored", b, NG * NU, g * NU + u + 1)
                        V.tensor_reduce(nmp[:, hh, i, part:part + 1], PS[:, a_banks(g)[u % len(a_banks(g))], 0:w], AX.X, ALU.max).then_inc(s["a_maxed"], 1)
                    elif kind == "N":
                        W(dve, "a_maxed", b, NG * NU, (g + 1) * NU)
                        W(dve, "nsT_done", b, 2 * NG, 2 * g)
                        step.did(V.tensor_reduce(nm[:, :, :].rearrange("p i h -> p h i"), nmp[:, :, :, :], AX.X, ALU.max))
                        step.did(V.tensor_scalar(nm[:, :, :], nm[:, :, :], -1.0, None, ALU.mult))
                        step.did(V.tensor_copy(nmb[:, :, :], nm[:, :, :]))
                        V.tensor_copy(ns[:, :, 0, :], nmb[:, :, :])
                        step.did(V.tensor_tensor(nmr[:, :, :], nm[:, :, :], nmb[:, :, :], ALU.subtract))
                        step.did(V.tensor_copy(nmb[:, :, :], nmr[:, :, :]))
                        V.tensor_copy(ns[:, :, 1, :], nmb[:, :, :])
                        V.tensor_tensor(ns[:, :, 2, :], nmr[:, :, :], nmb[:, :, :], ALU.subtract).then_inc(s["ns_ready"], 1)
                    elif kind == "STATS":
                        if more:
                            norm_stats((b + 1) * TB, 0)
                    elif kind == "R":
                        W(dve, "v_evac", b, TB, TB)
                        step.did(V.tensor_reduce(lmax[:, :], LG[:, :, :], AX.X, ALU.max))
                        V.tensor_tensor(LP[:, :, :], LG[:, :, :], lmax[:, :].unsqueeze(2).to_broadcast([P, TB, E]),
                                        ALU.subtract).then_inc(s["lshifted"], 1)
                        W(dve, "lprobs_ready", b, 1, 1)
                        step.did(V.tensor_reduce(lsum[:, :], LP[:, :, :], AX.X, ALU.add))
                        step.did(V.reciprocal(lmax[:, :], lsum[:, :]))
                        step.did(V.tensor_tensor(LP[:, :, :], LP[:, :, :], lmax[:, :].unsqueeze(2).to_broadcast([P, TB, E]), ALU.mult))
                        V.memset(pause[:, :], 0.0)
                        for j in range(TB):
                            i = V.max(top8[:, j, :], LP[:, j, :])
                        step.did(i)
                        step.did(V.tensor_copy(rep8[:, :, 0:2], top8[:, :, 0:2]))
                        V.memset(pause[:, :], 0.0)
                        for j in range(TB):
                            i = V.match_replace(out=CMB[:, j, :], in_to_replace=rep8[:, j, :], in_values=LP[:, j, :], imm_value=0.0)
                        step.did(i)
                        V.tensor_tensor(CMB[:, :, :], LP[:, :, :], CMB[:, :, :], ALU.subtract).then_inc(s["cmb_ready"], 1)
                    elif kind == "CT":
                        k = 2 * g + u
                        W(dve, "ctxT_done", b, 2 * NG, k + 1)
                        got = PS[:, 2, :].rearrange("p (q h e) -> p q h e", q=4, h=G4)
                        step.did(V.reciprocal(rc[:, :, :], got[:, :, :, DK]))
                        V.tensor_tensor(ctxN[:, 4 * u:4 * u + 4, g * G4 * DK:(g + 1) * G4 * DK].rearrange("p q (h d) -> p q h d", d=DK),
                                        got[:, :, :, 0:DK], rc[:, :, :].unsqueeze(3).to_broadcast([P, 4, G4, DK]),
                                        ALU.mult).then_inc(s["cn_done"], 1)
                    elif kind == "O2":
                        W(dve, "wohigh_ready", b, TB, u + 1)
                        low(cT[u % 2][:, 1, :, :], PS[:, output_banks(u)[0], 0:D].rearrange("p (k t) -> p k t", k=KD),
                            cT[u % 2][:, 0, :, :]).then_inc(s["wolow_ready"], 1)
                    elif kind == "O4":
                        W(dve, "wo_done", b, TB, u + 1)
                        V.tensor_tensor(xs[:, b * TB + u, :], PS[:, output_banks(u)[1], 0:D], xs[:, b * TB + u, :], ALU.add).then_inc(s["wo_added"], 1)

            def low_xb(b, j):
                W(dve, "bhigh_ready", b, TB, j + 1)
                t = slice(j * P, (j + 1) * P)
                low(xbT[:, 1, :, t], PS[:, 4 + j % 2, 0:D].rearrange("p (k t) -> p k t", k=KD), xbT[:, 0, :, t]).then_inc(s["blow2_ready"], 1)

            dve.wait_ge(s["rstd_ready"], 1)
            marks = [i for i, e in enumerate(TILES) if e[0] in ("H1", "H8")][:EA]
            for i, (kind, j) in enumerate(TILES):
                tile(kind, j, 0)
                if (kind, j) == ("H4", 0):
                    for n, (r, w) in enumerate(((wout_r, wout_s), (wkqv_r, wkqv_s), (wo_r, wo_s), (rw_r, rw_s[:, :, :]))):
                        dve.wait_ge(s["high_done"], n + 4)
                        i_low = low(r[:, 1, :, :], w, r[:, 0, :, :])
                    i_low.then_inc(s["rest_done"], 1)
                if i in marks and marks.index(i) % 2 == 0:
                    e = marks.index(i)
                    dve.wait_ge(s["ehigh_done"], e + 1)
                    low(ehl[0][:, 1, :, :], eraw[0], ehl[0][:, 0, :, :]).then_inc(elow_done[0], 1)
            dve.wait_ge(s["others_loaded"], 16 * (B - 1))
            for slot in range(2):
                dve.wait_ge(e_stored[slot], 16 * (EA // 2))
            per = 4 + 8 * 2 + NG * 5 + 7 + 2 * NG + 6 * TB
            with dve.Fori(0, B - 1) as b:
                step.enter(b, per)
                attention(b, True)
                dve.wait_ge(s["rstd_ready"], b * 2 + 3)
                both(b, BOTH)
                step.leave(B - 1, per)
            attention(B - 1, False)
            both(B - 1, EXPERTS)

        @block.scalar
        def _(act):
            A = nc.scalar

            def tile(kind, j, bt):
                sl = j % 2
                if kind == "T1":
                    W(act, "xT_done", bt, TB, j + 1)
                    W(act, "proj2_done", bt, TB, j - 1)
                    A.copy(xnT[sl][:, 0, :, :], PS[:, TILE, 0:D].rearrange("p (k t) -> p k t", k=KD)).then_inc(s["xhigh_ready"], 1)
                elif kind == "T2":
                    W(act, "proj1_done", bt, TB, j + 1)
                    W(act, "ctx_ready", bt, TB, j - 1)
                    W(act, "mulp_done", bt, 2 * TB, 2 * j - 2)
                    t = qkv[sl].rearrange("p h c d -> p (h c d)")
                    A.copy(t[:, 0:C], PS[:, TILE, :]).then_inc(s["half_ready"], 1)
                elif kind == "T3":
                    W(act, "proj2_done", bt, TB, j + 1)
                    t = qkv[sl].rearrange("p h c d -> p (h c d)")
                    A.copy(t[:, C:3 * D], PS[:, TILE, 0:3 * D - C]).then_inc(s["qkv_ready"], 1)
                    W(act, "leaf_ready", bt, TB, j - 1)
                    A.activation(gates[sl][:, 0:NODE], PS[:, TILE, D:D + NODE], ACT.Tanh, scale=0.5).then_inc(s["tanh_done"], 1)
                    W(act, "tanh_done", bt, TB, j + 1)
                    A.activation(gates[sl][:, 0:NODE], gates[sl][:, 0:NODE], ACT.Copy, scale=0.5, bias=0.5).then_inc(s["gate_ready"], 1)
                elif kind == "H5":
                    W(act, "shifted", bt, TB, j + 1)
                    W(act, "ctx_ready", bt, TB, j)
                    A.activation(prob, att, ACT.Exp, scale=SCALE).then_inc(s["probs_ready"], 1)
                elif kind == "K0":
                    W(act, "backT_done", bt, TB, j + 1)
                    W(act, "out_done", bt, TB, j - 1)
                    A.copy(clT[sl][:, 0, :, :], PS[:, TILE, :].rearrange("p (k t) -> p k t", k=4)).then_inc(s["chigh_ready"], 1)

            def expert(kind, q, b):
                if kind == "G":
                    W(act, "gu_done", b, 2 * NQ, 2 * q + 1)
                    W(act, "hs_ready", b, NQ, q - 1)
                    A.activation(SG[q % 2], PS[:, (2 * q) % 3, :], ACT.Silu).then_inc(s["silu_done"], 1)
                elif kind == "X":
                    W(act, "hf_ready", b, NQ, q + 1)
                    W(act, "y_done", b, NQ, q - 3)
                    A.copy(HR[q % 4][:, 0, :], HF[q % 2]).then_inc(s["hhigh_ready"], 1)

            def both(b, events):
                for kind, n in events:
                    if kind[0] in "THK":
                        tile(kind, n, b + 1)
                    else:
                        expert(kind, n, b)
                W(act, "y_done", b, NQ, NQ)
                A.copy(YT[:, 0, :, :], PS[:, ACC:ACC + 2, :])
                A.copy(YT[:, 1, :, :], PS[:, ACC + 2:ACC + 4, :]).then_inc(s["y_evac"], 1)

            def attention(b):
                for j in range(TB):
                    W(act, "lnT_done", b, TB, j + 1)
                    A.copy(xbT[:, 0, :, j * P:(j + 1) * P], PS[:, 4 + j % 2, 0:D].rearrange("p (k t) -> p k t", k=KD)).then_inc(s["bhigh_ready"], 1)
                for u in range(8):
                    W(act, "kq_done", b, 8, u + 1)
                    W(act, "parts_ready", b, 8, u - 1)
                    blk = KQ_ORDER[u // 2]
                    c = u % 2
                    A.activation(XF[u % 2], PS[:, u % 4, :], ACT.Identity, bias=bkq[:, blk:blk + 1])
                    A.activation(parts[:, blk, 0, c * C:(c + 1) * C], PS[:, u % 4, :], ACT.Identity,
                                 bias=bkq[:, blk:blk + 1]).then_inc(s["kq_evac"], 1)
                for j in range(TB):
                    W(act, "v_done", b, TB, j + 1)
                    if j == 0:
                        W(act, "aug_ready", b, 1, 1)
                    A.copy(vaug[:, j, :, 0:DK], PS[:, 4 + j % 2, 0:D].rearrange("p (h d) -> p h d", d=DK))
                    A.copy(LG[:, j, :], PS[:, 4 + j % 2, D:D + E]).then_inc(s["v_evac"], 1)
                for kind, g, u in ATTENTION:
                    if kind == "NT":
                        for c in range(2):
                            W(act, "nsT_done", b, 2 * NG, 2 * g + c + 1)
                            if c == 0 and g > 0:
                                W(act, neg[g - 1], b, 48 * (1 + (g == 1)), 48)
                            A.copy(NR[:, c * C:(c + 1) * C], PS[0:3 * G4, 2, :]).then_inc(s["nr_ready"], 1)
                    elif kind == "R":
                        W(act, "lshifted", b, 1, 1)
                        A.activation(LP[:, :, :], LP[:, :, :], ACT.Exp).then_inc(s["lprobs_ready"], 1)
                    elif kind == "RT":
                        for c in range(2):
                            W(act, "cmbT_done", b, 2, c + 1)
                            A.copy(cT8[:, c * C:(c + 1) * C], PS[0:E, 2, :]).then_inc(s["cmbT_ready"], 1)
                    elif kind in ("S0", "S1"):
                        w, p = q_span(*steps[u])[1], int(kind[1])
                        if p == 0:
                            W(act, "pv_done", b, NG * NS_, g * NS_ + u - 1)
                        W(act, "s_scored", b, 2 * NG * NS_, 2 * (g * NS_ + u) + p + 1)
                        A.activation(PT[u % 2][:, 2 * p:2 * p + 2, 0:w], PS[:, 3 + 2 * p:5 + 2 * p, 0:w], ACT.Exp,
                                     scale=SCALE).then_inc(s["p_ready"], 1)
                    elif kind == "CE":
                        k = 2 * g + u
                        W(act, "pv_done", b, NG * NS_, g * NS_ + (4 if u == 0 else NS_))
                        W(act, "ctxT_done", b, 2 * NG, k)
                        A.copy(CA, PS[:, 7, :]).then_inc(s["c_evac"], 1)
                    elif kind == "O1":
                        W(act, "woT_done", b, TB, u + 1)
                        W(act, "wo_done", b, TB, u - 1)
                        A.copy(cT[u % 2][:, 0, :, :], PS[:, output_banks(u)[0], 0:D].rearrange("p (k t) -> p k t", k=KD)).then_inc(s["wohigh_ready"], 1)

            act.wait_ge(s["bsum_ready"], 1)
            A.copy(bias_r[0:1, :], braw[:, 0:6 * D]).then_inc(s["high_done"], 1)
            act.wait_ge(s["wqkv_loaded"], 16)
            A.copy(wqkv_r[:, 0, :, :], wqkv_s).then_inc(s["high_done"], 1)
            act.wait_ge(s["fold_done"], 1)
            A.copy(rq_r[:, 0, :, :], PS[:, 0:2, 0:D])
            A.copy(lw_r[:, 0, :, :], PS[:, 2:4, 0:D]).then_inc(s["high_done"], 1)
            marks = [i for i, e in enumerate(TILES) if e[0] in ("H0", "H7")][:EA]
            for i, (kind, j) in enumerate(TILES):
                tile(kind, j, 0)
                if (kind, j) == ("T3", 0):
                    act.wait_ge(s["w_loaded"], 5 * 16)
                    for r, w in ((wout_r, wout_s), (wkqv_r, wkqv_s), (wo_r, wo_s), (rw_r, rw_s[:, :, :])):
                        A.copy(r[:, 0, :, :], w).then_inc(s["high_done"], 1)
                if i in marks:
                    e = marks.index(i)
                    act.wait_ge(eraw_loaded[e % 2], 48 * (e // 2 + 1))
                    if e >= 2:
                        act.wait_ge(e_stored[e % 2], 16 * (e // 2))
                    A.copy(ehl[e % 2][:, 0, :, :], eraw[e % 2]).then_inc(s["ehigh_done"], 1)
            for slot in range(2):
                act.wait_ge(e_stored[slot], 16 * (EA // 2))
            with act.Fori(0, B - 1) as b:
                attention(b)
                both(b, BOTH)
            attention(B - 1)
            both(B - 1, EXPERTS)

        @block.tensor
        def _(pe):
            M = nc.tensor

            def three(to, left, right, start, stop=True, blocks=range(KD)):
                passes = [(k, a, z) for k in blocks for a, z in ((0, 0), (0, 1), (1, 0))]
                for n, (k, a, z) in enumerate(passes):
                    last = M.matmul(to, left(a, k), right(z, k), start=start and n == 0, stop=stop and n + 1 == len(passes))
                return last

            def bias(to, at, n):
                M.matmul(to, ones_r[:, :], bias_r[:, at:at + n], start=True, stop=False)

            pe.wait_ge(s["folds_loaded"], 64)
            for bank, left, right in ((0, wq_s, rT_s), (2, lT_s, wwT_s)):
                for m in range(KD):
                    for k in range(KD):
                        last = M.matmul(PS[:, bank + m, 0:D], left[:, k, m * P:(m + 1) * P], right[:, k, :], start=k == 0, stop=k == KD - 1)
            last.then_inc(s["fold_done"], 1)
            pe.wait_ge(s["const_done"], 1)
            pe.wait_ge(s["consts_ready"], 1)
            pe.wait_ge(s["bias_ready"], 16)
            pe.wait_ge(s["ones_stored"], 16 * (NC_ + 1))
            pe.wait_ge(s["low_done"], 1)

            def tile(kind, j, bt):
                sl = j % 2
                if (kind, j) in TILE_USE:
                    n = TILE_USE[kind, j]
                    if n > 0:
                        before, i = USES[n - 1]
                        W(pe, LAST_READ[before], bt, TB, i + 1)
                if kind == "T1":
                    W(pe, "xn_ready", bt, TB, j + 1)
                    for k in range(KD):
                        last = M.transpose(PS[:, TILE, k * P:(k + 1) * P], xn[sl][:, k * P:(k + 1) * P], ident[:, :])
                    last.then_inc(s["xT_done"], 1)
                elif kind in ("T2", "T3"):
                    left = lambda a, k: xnT[sl][:, a, k, :]
                    if kind == "T2":
                        W(pe, "xlow_ready", bt, TB, j + 1)
                        bias(PS[:, TILE, :], BQKV, C)
                        three(PS[:, TILE, :], left, lambda z, k: wqkv_r[:, z, k, 0:C], False).then_inc(s["proj1_done"], 1)
                    else:
                        bias(PS[:, TILE, 0:D], BQKV + C, D)
                        three(PS[:, TILE, 0:D], left, lambda z, k: wqkv_r[:, z, k, C:3 * D], False)
                        three(PS[:, TILE, D:2 * D], left, lambda z, k: rq_r[:, z, k, :], True).then_inc(s["proj2_done"], 1)
                elif kind == "K0":
                    W(pe, "leaf_ready", bt, TB, j + 1)
                    W(pe, "ctx_ready", bt, TB, j + 1)
                    c, lf = ctx0[sl].rearrange("p h d -> p (h d)"), leaf[sl].rearrange("p n c -> p (n c)")
                    for k in range(4):
                        a = (c, lf)[k // 2]
                        last = M.transpose(PS[:, TILE, k * P:(k + 1) * P], a[:, k % 2 * P:(k % 2 + 1) * P], ident[:, :])
                    last.then_inc(s["backT_done"], 1)
                elif kind == "K1":
                    W(pe, "clow_ready", bt, TB, j + 1)
                    to = PS[:, TILE, 0:D]
                    bias(to, BOUT, D)
                    three(to, lambda a, k: clT[sl][:, a, k, :], lambda z, k: wout_r[:, z, k, :], False, stop=False)
                    three(to, lambda a, k: clT[sl][:, a, 2 + k, :], lambda z, k: lw_r[:, z, k, :], False).then_inc(s["out_done"], 1)

            def expert(kind, q, b):
                v, f = divmod(q, 2)
                e, c = divmod(v, 2)
                if kind in ("G", "U"):
                    n = 2 * q + (kind == "U")
                    if kind == "G" and q == 4 * e:
                        W(pe, ew[e % 2], b, 16 * 5, 16 * (e // 2 + 1))
                    if n >= 3:
                        W(pe, "hs_ready" if (n - 3) % 2 else "silu_done", b, NQ, (n - 3) // 2 + 1)
                    o = (n % 2) * FF + f * P
                    three(PS[:, n % 3, :], lambda a, k: ww[e % 2][:, a, k, o:o + P], lambda z, k: xbT[:, z, k, c * C:(c + 1) * C],
                          True).then_inc(s["gu_done"], 1)
                elif kind == "D":
                    W(pe, "hlow_ready", b, NQ, q + 1)
                    for m in range(KD):
                        last = three(PS[:, ACC + 2 * m + c, :], lambda a, k: ww[e % 2][:, a, k, 2 * FF + m * P:2 * FF + (m + 1) * P],
                                     lambda z, k: HR[q % 4][:, z, :], e == 0 and f == 0, stop=e == EA - 1 and f == 1, blocks=[f])
                    last.then_inc(s["y_done"], 1)

            def both(b, events):
                for kind, n in events:
                    if kind[0] in "THK":
                        tile(kind, n, b + 1)
                    else:
                        expert(kind, n, b)
                W(pe, "y_evac", b, 1, 1)
                for j in range(TB):
                    W(pe, "y_added", b, TB, j - 1)
                    for m in range(KD):
                        last = M.transpose(PS[:, j % 2, m * P:(m + 1) * P], YT[:, m, j // 4, (j % 4) * P:(j % 4 + 1) * P], ident[:, :])
                    last.then_inc(s["yT_done"], 1)

            def attention(b):
                for j in range(TB):
                    W(pe, "ln_ready", b, TB, j + 1)
                    W(pe, "blow2_ready", b, TB, j - 1)
                    for k in range(KD):
                        last = M.transpose(PS[:, 4 + j % 2, k * P:(k + 1) * P], xn2[j % 2][:, k * P:(k + 1) * P], ident[:, :])
                    last.then_inc(s["lnT_done"], 1)
                for u in range(8):
                    m, c = KQ_ORDER[u // 2], u % 2
                    if u == 0:
                        W(pe, "blow2_ready", b, TB, TB)
                    W(pe, "kq_evac", b, 8, u - 3)
                    three(PS[:, u % 4, :], lambda a, k: wkqv_r[:, a, k, m * P:(m + 1) * P], lambda z, k: xbT[:, z, k, c * C:(c + 1) * C],
                          True).then_inc(s["kq_done"], 1)
                for j in range(TB):
                    W(pe, "v_evac", b, TB, j - 1)
                    left = lambda a, k: xbT[:, a, k, j * P:(j + 1) * P]
                    to = PS[:, 4 + j % 2, 0:D]
                    bias(to, BV, D)
                    three(to, left, lambda z, k: wkqv_r[:, z, k, 2 * D:3 * D], False)
                    three(PS[:, 4 + j % 2, D:D + E], left, lambda z, k: rw_r[:, z, k, :], True).then_inc(s["v_done"], 1)
                W(pe, "kq_evac", b, 8, 8)

                for kind, g, u in ATTENTION:
                    Q, K = QS[g % 3], KS[g % 3]
                    if kind == "A":
                        hh, i, part = units[u]
                        w = min(C, (i + 1) * P - part * C)
                        if u == 0:
                            n = 16 * 2 * len(PAIRS)
                            W(pe, stack[g % 3], b, n + 16 + n * (g % 3 == 0), n + 16 + n * (g == 3))
                        if g == 0 and u == 0:
                            W(pe, "v_evac", b, TB, TB)
                        ring = a_banks(g)
                        W(pe, "a_maxed", b, NG * NU, g * NU + u - (len(ring) - 1))
                        bank = ring[u % len(ring)]
                        diag = (i + 1) * P - part * C <= C
                        last = M.matmul(PS[:, bank, 0:w], Q[0:ROWS, hh, i * P:(i + 1) * P], K[0:ROWS, hh, part * C:part * C + w],
                                        start=True, stop=not diag)
                        if diag:
                            last = M.matmul(PS[:, bank, w - P:w], identb[:, :], mask_n[:, :], start=False, stop=True)
                        last.then_inc(s["a_scored"], 1)
                    elif kind == "NT":
                        W(pe, "ns_ready", b, NG, g + 1)
                        W(pe, "cn_done", b, 2 * NG, 2 * (g - 1) + 1)
                        for c in range(2):
                            if c == 1:
                                W(pe, "nr_ready", b, 2 * NG, 2 * g + 1)
                            for j in range(4):
                                last = M.transpose(PS[0:3 * G4, 2, j * P:(j + 1) * P], ns[:, 4 * c + j, :, :].rearrange("p a h -> p (a h)"), ident[:, :])
                            last.then_inc(s["nsT_done"], 1)
                    elif kind == "RT":
                        W(pe, "cmb_ready", b, 1, 1)
                        W(pe, "nr_ready", b, 2 * NG, 2)
                        for c in range(2):
                            W(pe, "cmbT_ready", b, 2, c)
                            for j in range(4):
                                last = M.transpose(PS[0:E, 2, j * P:(j + 1) * P], CMB[:, 4 * c + j, :], ident[:, :])
                            last.then_inc(s["cmbT_done"], 1)
                    elif kind in ("S0", "S1"):
                        qc, kt = steps[u]
                        q0, w = q_span(qc, kt)
                        p = int(kind[1])
                        if u == 0 and p == 0:
                            W(pe, neg[g % 3], b, 48 * (1 + (g % 3 == 0)), 48 * (g // 3 + 1))
                        W(pe, "p_ready", b, 2 * NG * NS_, 2 * (g * NS_ + u) + p - 1)
                        for hh in (2 * p, 2 * p + 1):
                            diag = q0 == kt * P
                            last = M.matmul(PS[:, 3 + hh, 0:w], K[0:ROWS_M, hh, kt * P:(kt + 1) * P], Q[0:ROWS_M, hh, q0:q0 + w],
                                            start=True, stop=not diag)
                            if diag:
                                last = M.matmul(PS[:, 3 + hh, 0:P], identb[:, :], mask_t[:, :], start=False, stop=True)
                        last.then_inc(s["s_scored"], 1)
                    elif kind == "PV":
                        qc, kt = steps[u]
                        q0, w = q_span(qc, kt)
                        W(pe, "p_ready", b, 2 * NG * NS_, 2 * (g * NS_ + u) + 2)
                        if kt == 0:
                            W(pe, "c_evac", b, 2 * NG, 2 * g + qc)
                            if g == 0:
                                W(pe, "v_evac", b, TB, TB)
                        for hh in range(G4):
                            last = M.matmul(PS[32 * hh:32 * hh + 32, 7, q0 - qc * C:q0 - qc * C + w], vaug[:, kt, g * G4 + hh, :],
                                            PT[u % 2][:, hh, 0:w], start=kt == 0, stop=kt == 4 * qc + 3)
                        last.then_inc(s["pv_done"], 1)
                    elif kind == "CT":
                        k = 2 * g + u
                        W(pe, "c_evac", b, 2 * NG, k + 1)
                        W(pe, "cn_done", b, 2 * NG, k)
                        W(pe, "nr_ready", b, 2 * NG, 2 * min(NG, g + 1 + u))
                        W(pe, "cmbT_ready", b, 2, 2)
                        for j in range(4):
                            last = M.transpose(PS[:, 2, j * P:(j + 1) * P], CA[:, j * P:(j + 1) * P], ident[:, :])
                        last.then_inc(s["ctxT_done"], 1)
                    elif kind == "O1":
                        W(pe, "cn_done", b, 2 * NG, 2 * (NG - 1) + 1 + u // 4)
                        W(pe, "wolow_ready", b, TB, output_banks(u)[2])
                        for k in range(KD):
                            last = M.transpose(PS[:, output_banks(u)[0], k * P:(k + 1) * P], ctxN[:, u, k * P:(k + 1) * P], ident[:, :])
                        last.then_inc(s["woT_done"], 1)
                    elif kind == "O3":
                        W(pe, "wolow_ready", b, TB, u + 1)
                        W(pe, "wo_added", b, TB, output_banks(u)[2])
                        to = PS[:, output_banks(u)[1], 0:D]
                        bias(to, BO, D)
                        three(to, lambda a, k: cT[u % 2][:, a, k, :], lambda z, k: wo_r[:, z, k, :], False).then_inc(s["wo_done"], 1)
                W(pe, "wo_added", b, TB, TB)

            for kind, j in TILES:
                tile(kind, j, 0)
                if (kind, j) == ("H10", 0):
                    pe.wait_ge(s["rest_done"], 1)
            with pe.Fori(0, B - 1) as b:
                attention(b)
                both(b, BOTH)
            attention(B - 1)
            both(B - 1, EXPERTS)



def kernel(**inputs):
    import numpy as np
    import concourse.bacc as bacc
    from concourse.bass_utils import run_bass_kernel_spmd

    a = {k: np.asarray(v) for k, v in inputs.items()}
    blocks = lambda w: np.stack([w[:, i * FF:(i + 1) * FF] for i in range(ES)])
    laid = {
        "x": a["L0_attn_x"].reshape(N, D),
        "w_qkv": a["L0_attn_W_qkv"], "b_qkv": a["L0_attn_b_qkv"],
        "w_out": a["L0_attn_W_out"], "b_out0": a["L0_attn_b_out"],
        "wq": a["L0_ffn_Wq"], "routersT": np.pad(a["L0_ffn_routers"].T, ((0, 0), (0, 1))), "leafT": a["L0_ffn_leaf_values"].T,
        "woutT": a["L0_ffn_Wout_w"].T, "wout_b": a["L0_ffn_Wout_b"],
        "w_kqv": a["L1_attn_W_kqv"], "b_kqv": a["L1_attn_b_kqv"],
        "b_kq": a["L1_attn_b_kqv"][:2 * D].reshape(4, P).T,
        "w_o": a["L1_attn_W_o"], "b_o": a["L1_attn_b_o"], "router_w": a["L1_ffn_router_w"],
        "w_gate": np.concatenate([a["L1_ffn_gate_w"], blocks(a["L1_ffn_shared_gate_w"])]),
        "w_up": np.concatenate([a["L1_ffn_up_w"], blocks(a["L1_ffn_shared_up_w"])]),
        "w_down": np.concatenate([a["L1_ffn_down_w"], a["L1_ffn_shared_down_w"].reshape(ES, FF, D)]),
    }
    nc = bacc.Bacc("TRN2", target_bir_lowering=False, num_devices=1)
    laid = {k: np.ascontiguousarray(v) for k, v in laid.items()}
    aps = [nc.dram_tensor(f"in_{k}", v.shape, mybir.dt.from_np(v.dtype), kind="ExternalInput").ap() for k, v in laid.items()]
    out = nc.dram_tensor("out_0", (N, D), F32, kind="ExternalOutput").ap()
    build(nc, *aps, out)
    r = run_bass_kernel_spmd(nc, [{f"in_{k}": v for k, v in laid.items()}], core_ids=[0])
    return r.results[0]["out_0"].reshape(B, T, D)
```
